# Optimizing a Trainium2 kernel written in Bass

```python
import numpy as np
import jax
import jax.numpy as jnp

def _softmax(x, axis=-1):
    return jax.nn.softmax(x, axis=axis)

def _gelu(x):
    return jax.nn.gelu(x, approximate=True)

def _silu(x):
    return jax.nn.silu(x)

def _sigmoid(x):
    return jax.nn.sigmoid(x)

def _layernorm(x, axis=-1, eps=1e-05):
    m = jnp.mean(x, axis=axis, keepdims=True)
    v = jnp.var(x, axis=axis, keepdims=True)
    return (x - m) / jnp.sqrt(v + eps)

def _scatter_add(tgt, idx, src, axis=0):
    return tgt.at[idx].add(src)

def _segment_sum(src, seg, n):
    return jax.ops.segment_sum(src, seg, n)
kernel_name = 'mk_adaln_d2_jaxref_r4_fdcae8'

def setup_inputs(seed: int=0):
    np.random.seed(seed)
    _w = jnp.asarray

    def _L0_attn_setup():
        import jax, jax.numpy as jnp
        import numpy as np
        DIM = 512
        NUM_HEADS = 16
        HEAD_DIM = DIM // NUM_HEADS
        NEG = -10000.0
        key = jax.random.key(seed)
        k1, k2, k3, k4, k5 = jax.random.split(key, 5)
        B, S = (2, 512)
        x = jax.random.normal(k1, (B, S, DIM), dtype=jnp.float32)
        s = 1.0 / np.sqrt(DIM)
        W_qkv = jax.random.normal(k2, (DIM, 3 * DIM), dtype=jnp.float32) * s
        b_qkv = jax.random.normal(k3, (3 * DIM,), dtype=jnp.float32) * 0.01
        W_out = jax.random.normal(k4, (DIM, DIM), dtype=jnp.float32) * s
        b_out = jax.random.normal(k5, (DIM,), dtype=jnp.float32) * 0.01
        return {'x': x, 'W_qkv': W_qkv, 'b_qkv': b_qkv, 'W_out': W_out, 'b_out': b_out}
    _L0_attn_in = _L0_attn_setup()

    def _L0_ffn_setup():
        import jax, jax.numpy as jnp
        import numpy as np
        B, S, D, H = (4, 512, 512, 2048)

        def fwht(x):
            orig_shape = x.shape
            n = orig_shape[-1]
            x = x.reshape(-1, n)
            h = 1
            while h < n:
                xb = x.reshape(-1, n // (2 * h), 2, h)
                a = xb[:, :, 0, :]
                b = xb[:, :, 1, :]
                x = jnp.stack([a + b, a - b], axis=2).reshape(-1, n)
                h *= 2
            scale = jnp.asarray(1.0 / np.sqrt(n), dtype=x.dtype)
            return (x * scale).reshape(orig_shape)
        key = jax.random.key(seed)
        kx, k1, k2, k3 = jax.random.split(key, 4)
        x = jax.random.normal(kx, (B, S, D), dtype=jnp.float32)
        W1 = jax.random.normal(k1, (H, D), dtype=jnp.float32) * (1.0 / np.sqrt(D))
        W2 = jax.random.normal(k2, (D, H), dtype=jnp.float32) * (1.0 / np.sqrt(H))
        W3 = jax.random.normal(k3, (H, D), dtype=jnp.float32) * (1.0 / np.sqrt(D))
        return {'x': x, 'W1': W1, 'W2': W2, 'W3': W3}
    _L0_ffn_in = _L0_ffn_setup()
    _L0_c = _w((lambda *s: np.random.randn(*s).astype(np.float32) * 0.05)(1, 512))
    _L0_wmod = _w((lambda *s: np.random.randn(*s).astype(np.float32) * 0.05)(512, 6 * 512) * 512 ** (-0.5))

    def _L1_attn_setup():
        import jax, jax.numpy as jnp
        import numpy as np
        D_MODEL = 512
        N_HEADS = 16
        D_K = D_MODEL // N_HEADS
        EPS = 1e-06
        key = jax.random.key(seed)
        ks = jax.random.split(key, 9)
        s = 1.0 / np.sqrt(D_MODEL)
        return {'x': jax.random.normal(ks[0], (4, 1024, D_MODEL), dtype=jnp.float32), 'Wq': jax.random.normal(ks[1], (D_MODEL, D_MODEL), dtype=jnp.float32) * s, 'bq': jnp.zeros((D_MODEL,), dtype=jnp.float32), 'Wk': jax.random.normal(ks[2], (D_MODEL, D_MODEL), dtype=jnp.float32) * s, 'bk': jnp.zeros((D_MODEL,), dtype=jnp.float32), 'Wv': jax.random.normal(ks[3], (D_MODEL, D_MODEL), dtype=jnp.float32) * s, 'bv': jnp.zeros((D_MODEL,), dtype=jnp.float32), 'Wo': jax.random.normal(ks[4], (D_MODEL, D_MODEL), dtype=jnp.float32) * s, 'bo': jnp.zeros((D_MODEL,), dtype=jnp.float32)}
    _L1_attn_in = _L1_attn_setup()

    def _L1_ffn_setup():
        import jax, jax.numpy as jnp
        import numpy as np
        HIDDEN = 512
        INTER = 1408
        B, S = (2, 512)

        def _ternary(key, shape):
            return jax.random.randint(key, shape, -1, 2).astype(jnp.float32)
        key = jax.random.key(seed)
        ks = jax.random.split(key, 7)
        x = jax.random.normal(ks[0], (B, S, HIDDEN), dtype=jnp.float32)
        gate_w = _ternary(ks[1], (INTER, HIDDEN))
        up_w = _ternary(ks[2], (INTER, HIDDEN))
        down_w = _ternary(ks[3], (HIDDEN, INTER))
        gate_s = jax.random.uniform(ks[4], (INTER,), minval=0.01, maxval=0.1, dtype=jnp.float32)
        up_s = jax.random.uniform(ks[5], (INTER,), minval=0.01, maxval=0.1, dtype=jnp.float32)
        down_s = jax.random.uniform(ks[6], (HIDDEN,), minval=0.01, maxval=0.1, dtype=jnp.float32)
        return {'x': x, 'gate_w': gate_w, 'up_w': up_w, 'down_w': down_w, 'gate_s': gate_s, 'up_s': up_s, 'down_s': down_s}
    _L1_ffn_in = _L1_ffn_setup()
    _L1_c = _w((lambda *s: np.random.randn(*s).astype(np.float32) * 0.05)(1, 512))
    _L1_wmod = _w((lambda *s: np.random.randn(*s).astype(np.float32) * 0.05)(512, 6 * 512) * 512 ** (-0.5))
    _d = {'L0_attn_x': _L0_attn_in['x'], 'L0_attn_W_qkv': _L0_attn_in['W_qkv'], 'L0_attn_b_qkv': _L0_attn_in['b_qkv'], 'L0_attn_W_out': _L0_attn_in['W_out'], 'L0_attn_b_out': _L0_attn_in['b_out'], 'L0_ffn_W1': _L0_ffn_in['W1'], 'L0_ffn_W2': _L0_ffn_in['W2'], 'L0_ffn_W3': _L0_ffn_in['W3'], 'L0_c': _L0_c, 'L0_wmod': _L0_wmod, 'L1_attn_Wq': _L1_attn_in['Wq'], 'L1_attn_bq': _L1_attn_in['bq'], 'L1_attn_Wk': _L1_attn_in['Wk'], 'L1_attn_bk': _L1_attn_in['bk'], 'L1_attn_Wv': _L1_attn_in['Wv'], 'L1_attn_bv': _L1_attn_in['bv'], 'L1_attn_Wo': _L1_attn_in['Wo'], 'L1_attn_bo': _L1_attn_in['bo'], 'L1_ffn_gate_w': _L1_ffn_in['gate_w'], 'L1_ffn_up_w': _L1_ffn_in['up_w'], 'L1_ffn_down_w': _L1_ffn_in['down_w'], 'L1_ffn_gate_s': _L1_ffn_in['gate_s'], 'L1_ffn_up_s': _L1_ffn_in['up_s'], 'L1_ffn_down_s': _L1_ffn_in['down_s'], 'L1_c': _L1_c, 'L1_wmod': _L1_wmod}
    _x0 = _d['L0_attn_x']
    _d['L0_attn_x'] = jax.random.normal(jax.random.fold_in(jax.random.key(seed), 1), (1, 2048, 512), dtype=_x0.dtype)
    del _x0
    return _d

def reference(L0_attn_x, L0_attn_W_qkv, L0_attn_b_qkv, L0_attn_W_out, L0_attn_b_out, L0_ffn_W1, L0_ffn_W2, L0_ffn_W3, L0_c, L0_wmod, L1_attn_Wq, L1_attn_bq, L1_attn_Wk, L1_attn_bk, L1_attn_Wv, L1_attn_bv, L1_attn_Wo, L1_attn_bo, L1_ffn_gate_w, L1_ffn_up_w, L1_ffn_down_w, L1_ffn_gate_s, L1_ffn_up_s, L1_ffn_down_s, L1_c, L1_wmod):

    def _L0_attn_ref(x, W_qkv, b_qkv, W_out, b_out):
        import jax, jax.numpy as jnp
        import numpy as np
        DIM = 512
        NUM_HEADS = 16
        HEAD_DIM = DIM // NUM_HEADS
        NEG = -10000.0
        B, S, _ = x.shape
        qkv = x @ W_qkv + b_qkv
        qkv = qkv.reshape(B, S, NUM_HEADS, 3 * HEAD_DIM).transpose(0, 2, 1, 3)
        q, k, v = jnp.split(qkv, 3, axis=-1)
        scores = jnp.einsum('bhqd,bhkd->bhqk', q, k) / np.sqrt(HEAD_DIM)
        causal = jnp.tril(jnp.ones((S, S), dtype=bool))[None, None]
        scores = jnp.where(causal, scores, NEG)
        probs = jax.nn.softmax(scores, axis=-1)
        ctx = jnp.einsum('bhqk,bhkd->bhqd', probs, v)
        ctx = ctx.transpose(0, 2, 1, 3).reshape(B, S, DIM)
        return ctx @ W_out + b_out

    def _L0_ffn_ref(x, W1, W2, W3):
        import jax, jax.numpy as jnp
        import numpy as np
        B, S, D, H = (4, 512, 512, 2048)

        def fwht(x):
            orig_shape = x.shape
            n = orig_shape[-1]
            x = x.reshape(-1, n)
            h = 1
            while h < n:
                xb = x.reshape(-1, n // (2 * h), 2, h)
                a = xb[:, :, 0, :]
                b = xb[:, :, 1, :]
                x = jnp.stack([a + b, a - b], axis=2).reshape(-1, n)
                h *= 2
            scale = jnp.asarray(1.0 / np.sqrt(n), dtype=x.dtype)
            return (x * scale).reshape(orig_shape)
        up_gate = jnp.einsum('bsd,hd->bsh', x, W1)
        up_lin = jnp.einsum('bsd,hd->bsh', x, W3)
        hidden = jax.nn.silu(up_gate) * up_lin
        hidden = fwht(hidden)
        out = jnp.einsum('bsh,dh->bsd', hidden, W2)
        return out

    def _L1_attn_ref(x, Wq, bq, Wk, bk, Wv, bv, Wo, bo):
        import jax, jax.numpy as jnp
        import numpy as np
        D_MODEL = 512
        N_HEADS = 16
        D_K = D_MODEL // N_HEADS
        EPS = 1e-06
        b, n, _ = x.shape
        h, d = (N_HEADS, D_K)

        def proj(W, bias):
            y = jnp.einsum('bnm,dm->bnd', x, W) + bias
            return y.reshape(b, n, h, d).transpose(0, 2, 1, 3)
        Q = jax.nn.relu(proj(Wq, bq))
        K = jax.nn.relu(proj(Wk, bk))
        V = proj(Wv, bv)
        pos = jnp.arange(n, dtype=x.dtype)
        decay = jnp.exp(-pos / n)[None, None, :, None]
        Q = Q * decay
        K = K * decay
        KV = jnp.einsum('bhnd,bhne->bhde', K, V)
        Ksum = K.sum(axis=2)
        Z = 1.0 / (jnp.einsum('bhnd,bhd->bhn', Q, Ksum)[..., None] + EPS)
        out = jnp.einsum('bhnd,bhde->bhne', Q, KV) * Z
        out = out.transpose(0, 2, 1, 3).reshape(b, n, h * d)
        return jnp.einsum('bnm,dm->bnd', out, Wo) + bo

    def _L1_ffn_ref(x, gate_w, up_w, down_w, gate_s, up_s, down_s):
        import jax, jax.numpy as jnp
        import numpy as np
        HIDDEN = 512
        INTER = 1408
        B, S = (2, 512)

        def _ternary(key, shape):
            return jax.random.randint(key, shape, -1, 2).astype(jnp.float32)
        b, s, h = x.shape
        xf = x.reshape(b * s, h)
        g = jnp.einsum('th,ih->ti', xf, gate_w) * gate_s
        u = jnp.einsum('th,ih->ti', xf, up_w) * up_s
        hdn = jax.nn.silu(g) * u
        out = jnp.einsum('ti,hi->th', hdn, down_w) * down_s
        return out.reshape(b, s, -1)
    x = L0_attn_x
    mod = (_silu(L0_c) @ L0_wmod).reshape(L0_c.shape[0], 6, 1, -1)
    sa, ca, ga, sb, cb, gb = (mod[:, 0], mod[:, 1], mod[:, 2], mod[:, 3], mod[:, 4], mod[:, 5])
    ga = (2 * (ga >= 0) - 1) * jnp.maximum(jnp.abs(ga), 0.25)
    gb = (2 * (gb >= 0) - 1) * jnp.maximum(jnp.abs(gb), 0.25)
    h = _layernorm(x, axis=-1) * (1 + ca) + sa
    x = x + ga * _L0_attn_ref(h, L0_attn_W_qkv, L0_attn_b_qkv, L0_attn_W_out, L0_attn_b_out)
    h = _layernorm(x, axis=-1) * (1 + cb) + sb
    x = x + gb * _L0_ffn_ref(h, L0_ffn_W1, L0_ffn_W2, L0_ffn_W3)
    mod = (_silu(L1_c) @ L1_wmod).reshape(L1_c.shape[0], 6, 1, -1)
    sa, ca, ga, sb, cb, gb = (mod[:, 0], mod[:, 1], mod[:, 2], mod[:, 3], mod[:, 4], mod[:, 5])
    ga = (2 * (ga >= 0) - 1) * jnp.maximum(jnp.abs(ga), 0.25)
    gb = (2 * (gb >= 0) - 1) * jnp.maximum(jnp.abs(gb), 0.25)
    h = _layernorm(x, axis=-1) * (1 + ca) + sa
    x = x + ga * _L1_attn_ref(h, L1_attn_Wq, L1_attn_bq, L1_attn_Wk, L1_attn_bk, L1_attn_Wv, L1_attn_bv, L1_attn_Wo, L1_attn_bo)
    h = _layernorm(x, axis=-1) * (1 + cb) + sb
    x = x + gb * _L1_ffn_ref(h, L1_ffn_gate_w, L1_ffn_up_w, L1_ffn_down_w, L1_ffn_gate_s, L1_ffn_up_s, L1_ffn_down_s)
    return x

_drawn_inputs = setup_inputs


def setup_inputs(seed=0):
    import zlib

    import numpy as np

    out = dict(_drawn_inputs(seed))
    spreads = {'L1_attn_bq': (0.0, 0.8),
     'L1_attn_bk': (0.0, 0.8),
     'L1_attn_bv': (0.0, 0.313),
     'L1_attn_bo': (0.0, 0.324)}
    factors = {'L0_attn_b_qkv': 8.0,
     'L0_attn_b_out': 8.0,
     'L1_attn_Wq': 8.0,
     'L1_attn_Wk': 8.0,
     'L1_attn_Wv': 6.942}
    for name, (base, spread) in spreads.items():
        noise = np.random.default_rng([zlib.crc32(name.encode()), seed]).standard_normal(out[name].shape)
        drawn = base * np.exp(spread * noise) if base else spread * noise
        out[name] = jnp.asarray(drawn.astype(out[name].dtype))
    for name, factor in factors.items():
        out[name] = (out[name] * factor).astype(out[name].dtype)
    return out
```

```python
from contextlib import ExitStack

import concourse.bass as bass
from concourse import mybir

F32 = mybir.dt.float32
F32R = mybir.dt.float32r
BF16 = mybir.dt.bfloat16
ALU = mybir.AluOpType
ACT = mybir.ActivationFunctionType
AX_X = mybir.AxisListType.X

P = 128
S = 2048
D = 512
HEADS = 16
HD = D // HEADS
G = HEADS // 4
KT = D // P
T = S // P
NB = S // 512
TB = 512 // P
H0 = 2048
H1 = 1408
LN_EPS = 1e-5
Z_EPS = 1e-6
SCALE = float(HD) ** -0.5
MASKED = -32768.0
BIASROW = 3 * HD


def build_program(nc, a, out):
    with ExitStack() as whole:


        def sb(ctx, name, shape, dt=F32):
            return ctx.enter_context(nc.sbuf_tensor(name, shape, dt))

        held = {}

        def sem(ctx, name):
            def give_back():
                nc.clear_and_free_semaphores(held.pop(id(ctx)))
                nc.all_engine_barrier()
            if id(ctx) not in held:
                held[id(ctx)] = []
                if ctx is not whole:
                    ctx.callback(give_back)
            held[id(ctx)].append(nc.alloc_semaphore(name))
            return held[id(ctx)][-1]

        def dram(name, shape, dt=F32):
            return nc.dram_tensor(name, shape, dt).ap()

        stored = sem(whole, "output_stored")
        banks = whole.enter_context(nc.psum_tensor("banks", [P, 8, 512], F32))
        bank = [banks[:, i, :] for i in range(8)]

        ident = sb(whole, "ident", [P, P])
        ident16 = sb(whole, "ident16", [P, P], BF16)
        mask_keys = sb(whole, "mask_keys", [P, 2 * P], BF16)
        mask_queries = sb(whole, "mask_queries", [P, 2 * P], BF16)
        hadamard = sb(whole, "hadamard", [P, P], F32R)
        mod_cols = sb(whole, "mod_cols", [P, 2, 6, KT])
        gate_rows = sb(whole, "gate_rows", [P, 2, 2, D])
        tokens_a = sb(whole, "tokens_a", [P, T, D])
        tokens_b = sb(whole, "tokens_b", [P, T * D])
        x = tokens_a
        SA, CA, GA, SB, CB, GB = range(6)

        q_hi, q_lo, k_hi, k_lo = (dram(n, [G, P, S]) for n in ("q_hi", "q_lo", "k_hi", "k_lo"))
        mod_dram = dram("mod_dram", [2, 6, D])
        w2_mixed = dram("w2_mixed", [H0, D])
        z_dram = dram("z_dram", [P, 512])
        max_dram = dram("max_dram", [2, 2 * 4 * TB, P])

        def tile_rows(ap):
            return ap.rearrange("(t p) d -> p t d", p=P)

        class Norm:

            def __init__(self, ctx, tag, src, shift, scale, ht_hi, ht_lo, used=None, zbufs=2):
                self.used = used
                self.src, self.shift, self.scale, self.ht = src, shift, scale, (ht_hi, ht_lo)
                self.stats = sb(ctx, tag + "stats", [P, TB, 6])
                self.mv = sb(ctx, tag + "mv", [P, 2, TB, 2])
                self.ve = sb(ctx, tag + "ve", [P, 2, TB])
                self.std = sb(ctx, tag + "std", [P, 2, TB])
                self.rstd = sb(ctx, tag + "rstd", [P, 2, TB])
                self.zbufs = zbufs
                self.z = sb(ctx, tag + "z", [P, zbufs, TB, D])
                self.h = sb(ctx, tag + "h", [P, 2, 512])
                self.stats_done = sem(ctx, tag + "stats_done")
                self.std_done = sem(ctx, tag + "std_done")
                self.z_ready = sem(ctx, tag + "z_ready")
                self.turned = sem(ctx, tag + "turned")
                self.h_ready = sem(ctx, tag + "h_ready")
                self.hi_ready = sem(ctx, tag + "hi_ready")
                self.ht_ready = sem(ctx, tag + "ht_ready")

            def cols(self, b):
                at = 512 * (b % 2 if self.used else b)
                return slice(at, at + 512)

            def stats_vector(self, dve, b):
                q, base = b % 2, 10 * b
                for t in range(TB):
                    nc.vector.bn_stats(self.stats[:, t, :], self.src(b, t)).then_inc(self.stats_done, 1)
                for t in range(TB):
                    dve.wait_ge(self.stats_done, base + t + 1)
                    nc.vector.bn_aggr(self.mv[:, q, t, :], self.stats[:, t, :]).then_inc(self.stats_done, 1)
                dve.wait_ge(self.stats_done, base + 8)
                nc.vector.tensor_scalar(self.ve[:, q, :], self.mv[:, q, :, 1], LN_EPS, None,
                                        ALU.add).then_inc(self.stats_done, 1)

            def std_scalar(self, act, b):
                q = b % 2
                act.wait_ge(self.stats_done, 10 * b + 9)
                nc.scalar.activation(self.std[:, q, :], self.ve[:, q, :], ACT.Sqrt).then_inc(self.std_done, 1)

            def z_vector(self, dve, b):
                q = b % 2
                dve.wait_ge(self.std_done, b + 1)
                nc.vector.reciprocal(self.rstd[:, q, :], self.std[:, q, :]).then_inc(self.stats_done, 1)
                dve.wait_ge(self.stats_done, 10 * b + 10)
                if b >= self.zbufs:
                    dve.wait_ge(self.turned, KT * (b - self.zbufs + 1))
                for t in range(TB):
                    nc.vector.tensor_scalar(self.z[:, b % self.zbufs, t, :], self.src(b, t), self.mv[:, q, t, 0:1],
                                            self.rstd[:, q, t:t + 1], ALU.subtract,
                                            ALU.mult).then_inc(self.z_ready, 1)

            def tensor(self, pe, b):
                pe.wait_ge(self.z_ready, TB * (b + 1))
                for k in range(KT):
                    i = KT * b + k
                    if i >= 2:
                        pe.wait_ge(self.h_ready, i - 1)
                    for t in range(TB):
                        last = nc.tensor.transpose(bank[i % 2][:, t * P:(t + 1) * P],
                                                   self.z[:, b % self.zbufs, t, k * P:(k + 1) * P], ident[:])
                    last.then_inc(self.turned, 1)

            def h_scalar(self, act, b):
                for k in range(KT):
                    i = KT * b + k
                    act.wait_ge(self.turned, i + 1)
                    if i >= 2:
                        act.wait_ge(self.ht_ready, i - 1)
                    nc.scalar.activation(self.h[:, i % 2, :], bank[i % 2][:], ACT.Identity,
                                         bias=self.shift[:, k:k + 1],
                                         scale=self.scale[:, k:k + 1]).then_inc(self.h_ready, 1)

            def split_vector(self, dve, b):
                for k in range(KT):
                    i, cols = KT * b + k, self.cols(b)
                    if self.used and b >= 2 and k == 0:
                        self.used(dve, b)
                    dve.wait_ge(self.h_ready, i + 1)
                    nc.vector.tensor_copy(self.ht[0][:, k, cols], self.h[:, i % 2, :]).then_inc(self.hi_ready, 1)
                    dve.wait_ge(self.hi_ready, i + 1)
                    nc.vector.tensor_tensor(self.ht[1][:, k, cols], self.h[:, i % 2, :],
                                            self.ht[0][:, k, cols], ALU.subtract).then_inc(self.ht_ready, 1)

        def product(dst, lhs, rhs, n, first=True, last=True):
            for i in range(n):
                lh, ll = lhs(i)
                rh, rl = rhs(i)
                nc.tensor.matmul(dst, lh, rh, start=(first and i == 0), stop=False)
                nc.tensor.matmul(dst, lh, rl, start=False, stop=False)
                mm = nc.tensor.matmul(dst, ll, rh, start=False, stop=(last and i == n - 1))
            return mm

        with ExitStack() as ctx:
            x0 = tokens_b[:, :].rearrange("p (t d) -> p t d", t=T)
            v = tokens_a
            with ExitStack() as mods:
                wmod = sb(mods, "wmod", [P, 2, KT, 3 * D])
                ccol = sb(mods, "ccol", [P, 2, KT])
                csilu = sb(mods, "csilu", [P, 2, KT])
                cwide = sb(mods, "cwide", [P, 2, KT, 32])
                mod_rows = sb(mods, "mod_rows", [P, 4, D])
                stage = sb(mods, "const_stage", [P, 8 * P])
                gate_sign = sb(mods, "gate_sign", [P, 4, D])
                gate_abs = sb(mods, "gate_abs", [P, 4, D])
                c_loaded = sem(mods, "c_loaded")
                const_loaded = sem(mods, "const_loaded")
                wmod_loaded = [sem(mods, f"wmod_loaded{i}") for i in range(2)]
                csilu_ready = sem(mods, "csilu_ready")
                cwide_ready = sem(mods, "cwide_ready")
                mod_done = sem(mods, "mod_done")
                rows_ready = sem(mods, "rows_ready")
                rows_stored = sem(mods, "rows_stored")
                cols_loaded = sem(mods, "cols_loaded")
                gates_loaded = sem(mods, "gates_loaded")
                const_ready = sem(mods, "const_ready")
                gate_steps = sem(mods, "gate_steps")
                with nc.Block() as block:
                    @block.sync
                    def _(sp):
                        sp.dma_start(ccol[:, 0, :], a["L0_c"]).then_inc(c_loaded, 16)
                        sp.dma_start(ccol[:, 1, :], a["L1_c"]).then_inc(c_loaded, 16)
                        for i in range(4):
                            if i >= 2:
                                sp.wait_ge(mod_done, i - 1)
                            w = a[("L0_wmod", "L1_wmod")[i // 2]][:, (i % 2) * 3 * D:(i % 2 + 1) * 3 * D]
                            sp.dma_start(wmod[:, i % 2, :, :], tile_rows(w)).then_inc(wmod_loaded[i % 2], 16)
                            if i == 0:
                                sp.dma_start(stage[:], a["const"]).then_inc(const_loaded, 16)
                        for i in range(4):
                            sp.wait_ge(rows_ready, i + 1)
                            sp.dma_start(mod_dram[i // 2, 3 * (i % 2):3 * (i % 2) + 3, :],
                                         mod_rows[0:96:32, i, :]).then_inc(rows_stored, 16)
                        sp.wait_ge(rows_stored, 64)
                        for i in range(2):
                            for vec in range(6):
                                sp.dma_start(mod_cols[:, i, vec, :],
                                             mod_dram[i, vec, :].rearrange("(k p) -> p k", p=P),
                                             allow_slow_non_contiguous=True).then_inc(cols_loaded, 16)
                            for j, vec in enumerate((GA, GB)):
                                sp.dma_start(gate_rows[:, i, j, :],
                                             mod_dram[i, vec:vec + 1, :].broadcast_to([P, D])).then_inc(gates_loaded, 16)

                    @block.scalar
                    def _(act):
                        act.wait_ge(c_loaded, 32)
                        nc.scalar.activation(csilu[:], ccol[:], ACT.Silu).then_inc(csilu_ready, 1)

                    @block.tensor
                    def _(pe):
                        pe.wait_ge(cwide_ready, 1)
                        for i in range(4):
                            pe.wait_ge(wmod_loaded[i % 2], 16 * (i // 2 + 1))
                            for k in range(KT):
                                for vec in range(3):
                                    last = nc.tensor.matmul(bank[i][32 * vec:32 * vec + 32, :],
                                                            cwide[:, i // 2, k, :],
                                                            wmod[:, i % 2, k, vec * D:(vec + 1) * D],
                                                            start=(k == 0), stop=(k == KT - 1))
                            last.then_inc(mod_done, 1)

                    @block.vector
                    def _(dve):
                        dve.wait_ge(csilu_ready, 1)
                        nc.vector.tensor_copy(cwide[:], csilu[:].unsqueeze(3).broadcast_to([P, 2, KT, 32])).then_inc(cwide_ready, 1)
                        dve.wait_ge(const_loaded, 16)
                        nc.vector.tensor_copy(ident[:], stage[:, 0:P])
                        nc.vector.tensor_copy(ident16[:], stage[:, 0:P])
                        nc.vector.tensor_copy(hadamard[:], stage[:, P:2 * P])
                        nc.vector.tensor_copy(mask_keys[:], stage[:, 2 * P:4 * P])
                        nc.vector.tensor_copy(mask_queries[:], stage[:, 4 * P:6 * P]).then_inc(const_ready, 1)
                        for i in range(4):
                            dve.wait_ge(mod_done, i + 1)
                            nc.vector.tensor_copy(mod_rows[0:3 * 32, i, :], bank[i][0:3 * 32, :]).then_inc(rows_ready, 1)
                        dve.wait_ge(cols_loaded, 16 * 12)
                        for vec in (CA, CB):
                            nc.vector.tensor_scalar(mod_cols[:, :, vec, :], mod_cols[:, :, vec, :], 1.0, None, ALU.add)
                        dve.wait_ge(gates_loaded, 64)
                        rows = gate_rows[:].rearrange("p l g d -> p (l g) d")
                        nc.vector.tensor_scalar(gate_sign[:], rows, 0.0, 2.0, ALU.is_ge, ALU.mult).then_inc(gate_steps, 1)
                        nc.vector.tensor_scalar(gate_abs[:], rows, -1.0, None, ALU.mult).then_inc(gate_steps, 1)
                        dve.wait_ge(gate_steps, 2)
                        nc.vector.tensor_tensor(gate_abs[:], rows, gate_abs[:], ALU.max).then_inc(gate_steps, 1)
                        nc.vector.tensor_scalar(gate_sign[:], gate_sign[:], -1.0, None, ALU.add).then_inc(gate_steps, 1)
                        dve.wait_ge(gate_steps, 4)
                        nc.vector.tensor_scalar(gate_abs[:], gate_abs[:], 0.25, None, ALU.max).then_inc(gate_steps, 1)
                        dve.wait_ge(gate_steps, 5)
                        nc.vector.tensor_tensor(rows, gate_sign[:], gate_abs[:], ALU.mult)

            ht_hi = sb(ctx, "ht_hi", [P, KT, 2 * 512], F32R)
            ht_lo = sb(ctx, "ht_lo", [P, KT, 2 * 512], F32R)
            w_hi = sb(ctx, "qkv_w_hi", [P, 3, KT, D], F32R)
            w_lo = sb(ctx, "qkv_w_lo", [P, 3, KT, D], F32R)
            w_raw = sb(ctx, "qkv_w_raw", [P, KT, D])
            bias_cols = sb(ctx, "qk_bias", [P, 2 * G])
            bias_v = sb(ctx, "v_bias", [P, D])
            out_hi = sb(ctx, "qk_out_hi", [P, 2, 512], F32R)
            out_lo = sb(ctx, "qk_out_lo", [P, 2, 512], F32R)
            x_loaded = [sem(ctx, f"x_loaded{b}") for b in range(NB)]
            w_loaded = sem(ctx, "w_loaded")
            bias_loaded = sem(ctx, "bias_loaded")
            w_hi_ready = sem(ctx, "w_hi_ready")
            w_ready = sem(ctx, "w_ready")
            qkv_done = sem(ctx, "qkv_done")
            qk_hi_ready = sem(ctx, "qk_hi_ready")
            qkv_out = sem(ctx, "qkv_out")
            qk_lo_ready = sem(ctx, "qk_lo_ready")
            qk_stored = [sem(ctx, f"qk_stored{i}") for i in range(2)]
            norm = Norm(ctx, "n1_", lambda b, t: x0[:, TB * b + t, :], mod_cols[:, 0, SA, :],
                        mod_cols[:, 0, CA, :], ht_hi, ht_lo,
                        used=lambda dve, b: dve.wait_ge(qkv_done, (2 * G + TB) * (b - 1)))
            PER = 2 * G + TB
            with nc.Block() as block:
                @block.sync
                def _(sp):
                    xt = tile_rows(a["L0_attn_x"])
                    sp.dma_start(x0[:, 0:TB, :], xt[:, 0:TB, :]).then_inc(x_loaded[0], 16)
                    sp.dma_start(bias_cols[:], a["qk_bias"]).then_inc(bias_loaded, 16)
                    sp.dma_start(bias_v[:], a["v_bias"].broadcast_to([P, D])).then_inc(bias_loaded, 16)
                    for i in range(3):
                        if i:
                            sp.wait_ge(w_ready, i)
                        sp.dma_start(w_raw[:], tile_rows(a["w_qkv"][i])).then_inc(w_loaded, 16)
                        b = i + 1
                        sp.dma_start(x0[:, TB * b:TB * b + TB, :], xt[:, TB * b:TB * b + TB, :]).then_inc(x_loaded[b], 16)
                    for e in range(NB * 2 * G):
                        b, m = e // (2 * G), e % (2 * G)
                        hi, lo = ((q_hi, q_lo), (k_hi, k_lo))[m // G]
                        cols = slice(512 * b, 512 * b + 512)
                        sp.wait_ge(qk_hi_ready, e + 1)
                        sp.dma_start(hi[m % G, :, cols], out_hi[:, e % 2, :].bitcast(F32)).then_inc(qk_stored[e % 2], 16)
                        sp.wait_ge(qk_lo_ready, e + 1)
                        sp.dma_start(lo[m % G, :, cols], out_lo[:, e % 2, :].bitcast(F32)).then_inc(qk_stored[e % 2], 16)
                    for i in range(2):
                        sp.wait_ge(qk_stored[i], 32 * NB * G)

                @block.tensor
                def _(pe):
                    def qkv(b):
                        pe.wait_ge(norm.ht_ready, KT * (b + 1))
                        cols = norm.cols(b)
                        for m in range(PER):
                            n = PER * b + m
                            if b == 0 and m % G == 0:
                                pe.wait_ge(w_ready, m // G + 1)
                            if n >= 4:
                                pe.wait_ge(qkv_out, n - 3)
                            dst = bank[2 + n % 4][:]
                            if m < 2 * G:
                                i, c = m // G, slice(P * (m % G), P * (m % G) + P)
                                mm = product(dst, lambda k: (w_hi[:, i, k, c], w_lo[:, i, k, c]),
                                             lambda k: (ht_hi[:, k, cols], ht_lo[:, k, cols]), KT)
                            else:
                                at = cols.start + P * (m - 2 * G)
                                c = slice(at, at + P)
                                mm = product(dst, lambda k: (ht_hi[:, k, c], ht_lo[:, k, c]),
                                             lambda k: (w_hi[:, 2, k, :], w_lo[:, 2, k, :]), KT)
                            mm.then_inc(qkv_done, 1)
                    norm.tensor(pe, 0)
                    for b in range(NB):
                        if b + 1 < NB:
                            norm.tensor(pe, b + 1)
                        qkv(b)

                @block.scalar
                def _(act):
                    def qk_hi(b):
                        if b == 0:
                            act.wait_ge(bias_loaded, 32)
                        for m in range(2 * G):
                            e = 2 * G * b + m
                            act.wait_ge(qkv_done, PER * b + m + 1)
                            if e >= 2:
                                act.wait_ge(qk_stored[e % 2], 32 * (e // 2))
                            nc.scalar.activation(out_hi[:, e % 2, :], bank[2 + (PER * b + m) % 4][:], ACT.Identity,
                                                 bias=bias_cols[:, m:m + 1]).then_inc(qk_hi_ready, 1)
                    def weights(i):
                        act.wait_ge(w_loaded, 16 * (i + 1))
                        nc.scalar.copy(w_hi[:, i, :, :], w_raw[:]).then_inc(w_hi_ready, 1)
                    norm.std_scalar(act, 0)
                    weights(0)
                    norm.h_scalar(act, 0)
                    weights(1)
                    norm.std_scalar(act, 1)
                    weights(2)
                    for b in range(NB):
                        if b + 1 < NB:
                            norm.h_scalar(act, b + 1)
                        if b + 2 < NB:
                            norm.std_scalar(act, b + 2)
                        qk_hi(b)

                @block.vector
                def _(dve):
                    def qkv_rest(b):
                        if b == 0:
                            dve.wait_ge(bias_loaded, 32)
                        for m in range(PER):
                            n = PER * b + m
                            src = bank[2 + n % 4][:]
                            if m < 2 * G:
                                e = 2 * G * b + m
                                dve.wait_ge(qk_hi_ready, e + 1)
                                if e >= 2:
                                    dve.wait_ge(qk_stored[e % 2], 32 * (e // 2))
                                nc.vector.scalar_tensor_tensor(out=out_lo[:, e % 2, :], in0=src,
                                                               scalar=bias_cols[:, m:m + 1], in1=out_hi[:, e % 2, :],
                                                               op0=ALU.add, op1=ALU.subtract).then_inc(qkv_out, 1)
                                dve.wait_ge(qkv_out, n + 1)
                                dve.sem_inc(qk_lo_ready, 1)
                            else:
                                dve.wait_ge(qkv_done, n + 1)
                                nc.vector.tensor_tensor(v[:, TB * b + m - 2 * G, :], src, bias_v[:],
                                                        ALU.add).then_inc(qkv_out, 1)

                    def weights(i):
                        dve.wait_ge(w_hi_ready, i + 1)
                        nc.vector.tensor_tensor(w_lo[:, i, :, :], w_raw[:], w_hi[:, i, :, :],
                                                ALU.subtract).then_inc(w_ready, 1)
                    dve.wait_ge(x_loaded[0], 16)
                    norm.stats_vector(dve, 0)
                    norm.z_vector(dve, 0)
                    weights(0)
                    dve.wait_ge(x_loaded[1], 16)
                    norm.stats_vector(dve, 1)
                    norm.split_vector(dve, 0)
                    norm.z_vector(dve, 1)
                    weights(1)
                    weights(2)
                    for b in range(NB):
                        if b + 1 < NB:
                            norm.split_vector(dve, b + 1)
                        if b + 2 < NB:
                            dve.wait_ge(x_loaded[b + 2], 16)
                            norm.stats_vector(dve, b + 2)
                            norm.z_vector(dve, b + 2)
                        qkv_rest(b)

        ctx0 = tokens_b[:, :].rearrange("p (g t) -> p g t", g=G)
        with ExitStack() as ctx:
            v = tokens_a
            QS = 4
            kst = sb(ctx, "kst", [P, 2, 4, S], F32R)
            qst = sb(ctx, "qst", [P, QS, 4, 512], F32R)
            probs = sb(ctx, "probs", [P, 3, 2, 512])
            ones = sb(ctx, "ones", [P, HD])
            part_max = sb(ctx, "part_max", [P, 2, 4 * TB, NB])
            neg_max = sb(ctx, "neg_max", [P, 4 * TB])
            neg_hi = sb(ctx, "neg_hi", [P, 4 * TB], F32R)
            neg_parts = sb(ctx, "neg_parts", [P, 2 * 4 * TB])
            max_rows = sb(ctx, "max_rows", [2 * 4 * TB, 2, P], F32R)
            o_copy = sb(ctx, "o_copy", [P, 2, 512])
            sum_copy = sb(ctx, "sum_copy", [P, 2, 512])
            FW = 64
            fw = [sb(ctx, f"fw{i}", [P, H0 // P, FW]) for i in range(2)]
            NQ = G * NB
            k_loaded = [[sem(ctx, f"k_loaded{i}_{j}") for j in range(NB)] for i in range(2)]
            q_loaded = [sem(ctx, f"q_loaded{i}") for i in range(QS)]
            max_stored = [sem(ctx, f"max_stored{i}") for i in range(QS)]
            ones_ready = sem(ctx, "ones_ready")
            max_mm = sem(ctx, "max_mm")
            max_read = sem(ctx, "max_read")
            max_chain = sem(ctx, "max_chain")
            rows_ready = sem(ctx, "max_rows_ready")
            rows_stored = sem(ctx, "max_rows_stored")
            score_mm = sem(ctx, "score_mm")
            exp_done = sem(ctx, "exp_done")
            pv_done = sem(ctx, "pv_done")
            copied = sem(ctx, "copied")
            o_copied = sem(ctx, "o_copied")
            rec_done = sem(ctx, "rec_done")
            ctx_done = sem(ctx, "ctx_done")
            fw_loaded = sem(ctx, "fw_loaded")
            fw_step = sem(ctx, "fw_step")
            fw_stored = sem(ctx, "fw_stored")

            def slots_before(n):
                g, j = divmod(n, NB)
                return g * (4 * TB * NB * (NB + 1) // 2 + NB) + 4 * TB * j * (j + 1) // 2 + j

            def pairs_before(n):
                g, j = divmod(n, NB)
                return g * (2 * TB * NB * (NB + 1) // 2) + 2 * TB * j * (j + 1) // 2

            LEAD = 6
            PRELUDE = slots_before(1) + 10

            def schedule():
                done = PRELUDE
                goals = [(pairs_before(n) - LEAD, slots_before(n + 1)) for n in range(1, NQ)]
                turns = [goal - 1 for _, goal in goals]
                for n in range(NQ):
                    for i in range(pairs_before(n + 1) - pairs_before(n)):
                        at = pairs_before(n) + i
                        need = [-(-(goal - done) // max(by - at, 1)) for by, goal in goals if goal > done]
                        now = max([0] + need)
                        for turn in turns:
                            if done < turn < done + now:
                                now = turn - done
                            elif done == turn:
                                now = 1
                        yield n, i, range(done, done + now)
                        done += now

            def slot_of(slot):
                n = max(m for m in range(NQ) if slots_before(m) <= slot)
                return n, slot - slots_before(n)

            with nc.Block() as block:
                @block.sync
                def _(sp):
                    for n in range(NQ):
                        g, j = divmod(n, NB)
                        cols = slice(512 * j, 512 * j + 512)
                        if n >= QS:
                            sp.wait_ge(score_mm, 2 * pairs_before(n - QS + 1))
                        if g >= 2 and j == 0:
                            sp.wait_ge(score_mm, 2 * pairs_before(NB * (g - 1)))
                        for part, (qs, ks) in enumerate(((q_hi, k_hi), (q_hi, k_lo), (q_lo, k_hi))):
                            rows = slice(HD * part, HD * part + HD)
                            sp.dma_start(qst[rows, n % QS, :, :].bitcast(F32),
                                         qs[g, :, cols].rearrange("(h d) t -> d h t", h=4)).then_inc(q_loaded[n % QS], 16)
                            sp.dma_start(kst[rows, g % 2, :, cols].bitcast(F32),
                                         ks[g, :, cols].rearrange("(h d) t -> d h t", h=4)).then_inc(k_loaded[g % 2][j], 16)

                @block.gpsimd
                def _(pool):
                    w2 = a["w2t"].rearrange("(c p) d -> p c d", p=P)
                    w2m = w2_mixed.rearrange("(c p) d -> p c d", p=P)

                    def butterflies(s):
                        cols = slice(FW * s, FW * s + FW)
                        if s:
                            pool.wait_ge(fw_stored, 16 * s)
                        pool.dma_start(fw[0][:], w2[:, :, cols]).then_inc(fw_loaded, 16)
                        pool.wait_ge(fw_loaded, 16 * (s + 1))
                        for r in range(4):
                            half = 1 << r
                            src = fw[r % 2][:].rearrange("p (a b h) d -> p a b (h d)", b=2, h=half)
                            dst = fw[1 - r % 2][:].rearrange("p (a b h) d -> p a b (h d)", b=2, h=half)
                            nc.gpsimd.tensor_tensor(dst[:, :, 0, :], src[:, :, 0, :], src[:, :, 1, :], ALU.add).then_inc(fw_step, 1)
                            nc.gpsimd.tensor_tensor(dst[:, :, 1, :], src[:, :, 0, :], src[:, :, 1, :], ALU.subtract).then_inc(fw_step, 1)
                            pool.wait_ge(fw_step, 8 * s + 2 * r + 2)
                        pool.dma_start(w2m[:, :, cols], fw[0][:]).then_inc(fw_stored, 16)
                    for n in range(NQ):
                        pool.wait_ge(rows_ready, n + 1)
                        if n >= QS:
                            pool.wait_ge(score_mm, 2 * pairs_before(n - QS + 1))
                        pool.dma_start(max_dram[n % 2], max_rows[:, n % 2, :].bitcast(F32)).then_inc(rows_stored, 16)
                        pool.wait_ge(rows_stored, 16 * (n + 1))
                        pool.dma_start(qst[BIASROW:BIASROW + 2, n % QS, :, :].bitcast(F32),
                                       max_dram[n % 2].rearrange("(part h t) q -> part h (t q)", part=2, h=4)
                                       ).then_inc(max_stored[n % QS], 16)
                        if 2 <= n < 2 + D // FW:
                            butterflies(n - 2)
                    pool.wait_ge(fw_stored, 16 * (D // FW))

                @block.tensor
                def _(pe):
                    def max_step(n, i):
                        g, j = divmod(n, NB)
                        slot = slots_before(n) + i
                        dst = bank[slot % 3]
                        if i == 0:
                            pe.wait_ge(q_loaded[n % QS], 48 * (n // QS + 1))
                            pe.wait_ge(k_loaded[g % 2][j], 48 * (g // 2 + 1))
                        if slot >= 3:
                            pe.wait_ge(max_read, slot - 2)
                        if i == 4 * TB * (j + 1):
                            pe.wait_ge(max_chain, 4 * n + 4)
                            nc.tensor.transpose(dst[0:2 * 4 * TB, 0:P], neg_parts[:], ident[:]).then_inc(max_mm, 1)
                            return
                        ht, c = divmod(i, j + 1)
                        h, t = divmod(ht, TB)
                        wide = 512 if c < j else max(P * (t + 1), 2 * P)
                        mm = nc.tensor.matmul(dst[:, 0:wide], qst[0:BIASROW, n % QS, h, P * t:P * t + P],
                                              kst[0:BIASROW, g % 2, h, 512 * c:512 * c + wide],
                                              start=True, stop=(c < j))
                        if c == j:
                            at = P * t
                            mw = 2 * P if t == 0 else P
                            mm = nc.tensor.matmul(dst[:, at:at + mw], ident16[:], mask_queries[:, 0:mw],
                                                  start=False, stop=True)
                        mm.then_inc(max_mm, 1)

                    def score(n, i):
                        g, j = divmod(n, NB)
                        kt, pair = divmod(i, 2)
                        sp_ = pairs_before(n) + i
                        if i == 0:
                            pe.wait_ge(max_stored[n % QS], 16 * (n // QS + 1))
                        t = kt - TB * j
                        c0 = min(P * max(t, 0), 2 * P)
                        for u in range(2):
                            h = 2 * pair + u
                            sh = 2 * sp_ + u
                            dst = bank[3 + sh % 3]
                            if sh >= 3:
                                pe.wait_ge(exp_done, sh - 2)
                            mm = nc.tensor.matmul(dst[:, c0:512], kst[0:BIASROW + 2, g % 2, h, P * kt:P * kt + P],
                                                  qst[0:BIASROW + 2, n % QS, h, c0:512], start=True, stop=(t < 0))
                            if t >= 0:
                                mw = 2 * P if t == 3 else P
                                mm = nc.tensor.matmul(dst[:, c0:c0 + mw], ident16[:], mask_keys[:, 2 * P - mw:2 * P],
                                                      start=False, stop=True)
                            mm.then_inc(score_mm, 1)

                    def context(n, i):
                        g, j = divmod(n, NB)
                        kt, pair = divmod(i, 2)
                        sp_ = pairs_before(n) + i
                        if i == 0 and n:
                            pe.wait_ge(copied, 2 * n)
                            pe.wait_ge(o_copied, n)
                        pe.wait_ge(exp_done, 2 * sp_ + 2)
                        c0 = min(P * max(kt - TB * j, 0), 2 * P)
                        first, last = kt == 0, kt == TB * (j + 1) - 1
                        for u in range(2):
                            h = 2 * pair + u
                            nc.tensor.matmul(bank[6][HD * h:HD * h + HD, c0:512],
                                             v[:, kt, HD * (4 * g + h):HD * (4 * g + h) + HD],
                                             probs[:, sp_ % 3, u, c0:512], start=first, stop=last)
                        for u in range(2):
                            h = (2 * pair + u + 2) % 4
                            mm = nc.tensor.matmul(bank[7][HD * h:HD * h + HD, c0:512], ones[:],
                                                  probs[:, sp_ % 3, u, c0:512], start=first, stop=last)
                        mm.then_inc(pv_done, 1)

                    pe.wait_ge(ones_ready, 2)
                    for slot in range(PRELUDE):
                        max_step(*slot_of(slot))
                    late = None
                    for n, i, slots in schedule():
                        first = len(slots) // 2
                        score(n, i)
                        for slot in slots[:first]:
                            max_step(*slot_of(slot))
                        if late:
                            context(*late)
                        for slot in slots[first:]:
                            max_step(*slot_of(slot))
                        late = (n, i)
                    context(*late)

                @block.scalar
                def _(act):
                    def copies(n):
                        act.wait_ge(pv_done, pairs_before(n + 1))
                        if n >= 2:
                            act.wait_ge(ctx_done, 4 * (n - 1))
                        nc.scalar.copy(sum_copy[0:64, n % 2, :], bank[7][64:128, :]).then_inc(copied, 1)
                        nc.scalar.copy(sum_copy[64:128, n % 2, :], bank[7][0:64, :]).then_inc(copied, 1)
                    for n in range(NQ):
                        j = n % NB
                        for i in range(pairs_before(n + 1) - pairs_before(n)):
                            sp_ = pairs_before(n) + i
                            c0 = min(P * max(i // 2 - TB * j, 0), 2 * P)
                            if sp_ >= 3:
                                act.wait_ge(pv_done, sp_ - 2)
                            for u in range(2):
                                sh = 2 * sp_ + u
                                act.wait_ge(score_mm, sh + 1)
                                nc.scalar.activation(probs[:, sp_ % 3, u, c0:512], bank[3 + sh % 3][:, c0:512],
                                                     ACT.Exp, scale=SCALE).then_inc(exp_done, 1)
                            if i == 0 and n:
                                copies(n - 1)
                    copies(NQ - 1)

                @block.vector
                def _(dve):
                    nc.vector.memset(kst[BIASROW:BIASROW + 2, :, :, :].bitcast(F32), 1.0).then_inc(ones_ready, 1)
                    nc.vector.memset(ones[:], 1.0).then_inc(ones_ready, 1)

                    def max_step(n, i):
                        g, j = divmod(n, NB)
                        slot = slots_before(n) + i
                        if i == 4 * TB * (j + 1):
                            parts = 4 * TB
                            dve.wait_ge(max_read, slot)
                            nc.vector.tensor_reduce(neg_max[:], part_max[:, n % 2, :, 0:j + 1], AX_X, ALU.max,
                                                    negate=True).then_inc(max_chain, 1)
                            dve.wait_ge(max_chain, 4 * n + 1)
                            nc.vector.tensor_copy(neg_hi[:], neg_max[:]).then_inc(max_chain, 1)
                            dve.wait_ge(max_chain, 4 * n + 2)
                            nc.vector.tensor_copy(neg_parts[:, 0:parts], neg_hi[:]).then_inc(max_chain, 1)
                            nc.vector.tensor_tensor(neg_parts[:, parts:2 * parts], neg_max[:], neg_hi[:],
                                                    ALU.subtract).then_inc(max_chain, 1)
                            dve.wait_ge(max_mm, slot + 1)
                            if n >= 2:
                                dve.wait_ge(max_stored[(n - 2) % QS], 16 * ((n - 2) // QS + 1))
                            nc.vector.tensor_copy(max_rows[:, n % 2, :], bank[slot % 3][0:2 * parts, 0:P]).then_inc(max_read, 1)
                            dve.wait_ge(max_read, slot + 1)
                            dve.sem_inc(rows_ready, 1)
                            return
                        ht, c = divmod(i, j + 1)
                        t = ht % TB
                        wide = 512 if c < j else max(P * (t + 1), 2 * P)
                        dve.wait_ge(max_mm, slot + 1)
                        nc.vector.tensor_reduce(part_max[:, n % 2, ht, c:c + 1], bank[slot % 3][:, 0:wide], AX_X,
                                                ALU.max).then_inc(max_read, 1)

                    def normalise(n, part):
                        g, j = divmod(n, NB)
                        c = slice(P * part, P * part + P)
                        if part == 0:
                            dve.wait_ge(copied, 2 * n + 2)
                        nc.vector.reciprocal(sum_copy[:, n % 2, c], sum_copy[:, n % 2, c]).then_inc(rec_done, 1)
                        dve.wait_ge(rec_done, 4 * n + part + 1)
                        nc.vector.tensor_tensor(ctx0[:, g, 512 * j + P * part:512 * j + P * part + P],
                                                o_copy[:, n % 2, c], sum_copy[:, n % 2, c],
                                                ALU.mult).then_inc(ctx_done, 1)

                    def copy_out(n):
                        dve.wait_ge(pv_done, pairs_before(n + 1))
                        if n >= 2:
                            dve.wait_ge(ctx_done, 4 * (n - 1))
                        nc.vector.tensor_copy(o_copy[:, n % 2, :], bank[6][:]).then_inc(o_copied, 1)

                    for slot in range(PRELUDE):
                        max_step(*slot_of(slot))
                    for n, i, slots in schedule():
                        first = len(slots) // 2
                        for slot in slots[:first]:
                            max_step(*slot_of(slot))
                        if n and i == 0:
                            copy_out(n - 1)
                        for slot in slots[first:]:
                            max_step(*slot_of(slot))
                        if n and 2 <= i < 6:
                            normalise(n - 1, i - 2)
                    copy_out(NQ - 1)
                    for part in range(4):
                        normalise(NQ - 1, part)

        def project_out(ctx, tag, w, bias, gate, src, src_ready, res_ready, bufs=2):
            raw = sb(ctx, tag + "w_raw", [P, KT, D])
            bias_row = sb(ctx, tag + "bias", [P, D])
            w_hi = sb(ctx, tag + "w_hi", [P, KT, D], F32R)
            w_lo = sb(ctx, tag + "w_lo", [P, KT, D], F32R)
            c_hi = sb(ctx, tag + "c_hi", [P, bufs, G, 512], F32R)
            c_lo = sb(ctx, tag + "c_lo", [P, bufs, G, 512], F32R)
            loaded = sem(ctx, tag + "w_loaded")
            gated = sem(ctx, tag + "w_gated_s")
            bias_gated = sem(ctx, tag + "bias_gated")
            w_hi_s = sem(ctx, tag + "w_hi_s")
            w_ready = sem(ctx, tag + "w_ready")
            hi_s = sem(ctx, tag + "c_hi_s")
            c_ready = sem(ctx, tag + "c_ready")
            xb_ready = sem(ctx, tag + "xb_ready")
            proj = sem(ctx, tag + "proj")
            x_ready = sem(ctx, tag + "x_ready")

            class Parts:
                ready = x_ready

                def sync(sp):
                    sp.dma_start(raw[:], tile_rows(w)).then_inc(loaded, 16)
                    sp.dma_start(bias_row[:], bias.broadcast_to([P, D])).then_inc(loaded, 16)

                def weights_vector(dve):
                    dve.wait_ge(loaded, 32)
                    nc.vector.tensor_tensor(bias_row[:], bias_row[:], gate, ALU.mult).then_inc(bias_gated, 1)
                    nc.vector.tensor_tensor(raw[:], raw[:], gate.unsqueeze(1).broadcast_to([P, KT, D]),
                                            ALU.mult).then_inc(gated, 1)
                    dve.wait_ge(gated, 1)
                    nc.vector.tensor_copy(w_hi[:], raw[:]).then_inc(w_hi_s, 1)
                    dve.wait_ge(w_hi_s, 1)
                    nc.vector.tensor_tensor(w_lo[:], raw[:], w_hi[:], ALU.subtract).then_inc(w_ready, 1)

                def bias_gpsimd(pool):
                    pool.wait_ge(bias_gated, 1)
                    for t in range(T):
                        res_ready(pool, t)
                        nc.gpsimd.tensor_tensor(x[:, t, :], x[:, t, :], bias_row[:], ALU.add).then_inc(xb_ready, 1)

                def hi_scalar(act, b):
                    for g in range(G):
                        src_ready(act, b, g)
                        if b >= bufs:
                            act.wait_ge(proj, TB * (b - bufs + 1))
                        nc.scalar.copy(c_hi[:, b % bufs, g, :], src(b, g)).then_inc(hi_s, 1)

                def lo_vector(dve, b):
                    for g in range(G):
                        dve.wait_ge(hi_s, G * b + g + 1)
                        nc.vector.tensor_tensor(c_lo[:, b % bufs, g, :], src(b, g), c_hi[:, b % bufs, g, :],
                                                ALU.subtract).then_inc(c_ready, 1)

                def tensor(pe, b):
                    pe.wait_ge(w_ready, 1)
                    pe.wait_ge(c_ready, G * (b + 1))
                    for t in range(TB):
                        n = TB * b + t
                        if n >= 4:
                            pe.wait_ge(x_ready, n - 3)
                        c = slice(P * t, P * t + P)
                        product(bank[2 + n % 4][:], lambda g: (c_hi[:, b % bufs, g, c], c_lo[:, b % bufs, g, c]),
                                lambda g: (w_hi[:, g, :], w_lo[:, g, :]), G).then_inc(proj, 1)

                def add_vector(dve, b):
                    for t in range(TB):
                        n = TB * b + t
                        dve.wait_ge(proj, n + 1)
                        dve.wait_ge(xb_ready, n + 1)
                        nc.vector.tensor_tensor(x[:, n, :], bank[2 + n % 4][:], x[:, n, :], ALU.add).then_inc(x_ready, 1)
            return Parts

        def feed_forward(tag, layer, gate_w, up_w, down_w, hidden, ht, gate_s=None, up_s=None, down_s=None,
                         store=None):
            nch = hidden // P
            segs = [list(range(c, min(c + 2, nch))) for c in range(0, nch, 2)]
            mixed = down_s is None
            steps = [(s, b) for s in range(len(segs)) for b in range(NB)]
            ubase = [0]
            for s, b in steps:
                ubase.append(ubase[-1] + len(segs[s]))
            with ExitStack() as ctx:
                def part(at, outer, inner):
                    return tokens_b[:, at:at + outer * inner].rearrange("p (o i) -> p o i", o=outer)
                raw_g, raw_u = part(0, KT, 2 * P), part(1024, KT, 2 * P)
                raw_d, down = part(2048, 2, D), part(3072, 2, D)
                silu, act_ = part(4096, 2, 512), part(5120, 2, 512)
                drow = tokens_b[:, 6144:6144 + D]
                wh = [sb(ctx, tag + f"w{n}_hi", [P, 2, KT, 2 * P], F32R) for n in "gu"]
                wl = [sb(ctx, tag + f"w{n}_lo", [P, 2, KT, 2 * P], F32R) for n in "gu"]
                dh = sb(ctx, tag + "d_hi", [P, 2, 2, D], F32R)
                dl = sb(ctx, tag + "d_lo", [P, 2, 2, D], F32R)
                if not mixed:
                    gs = sb(ctx, tag + "gs", [P, nch])
                    us = sb(ctx, tag + "us", [P, nch])
                hh = sb(ctx, tag + "hid_hi", [P, 2, 2, 512], F32R)
                hl = sb(ctx, tag + "hid_lo", [P, 2, 2, 512], F32R)
                scales_loaded = sem(ctx, tag + "scales_loaded")
                drow_ready = sem(ctx, tag + "drow_ready")
                gu_loaded = sem(ctx, tag + "gu_loaded")
                d_loaded = sem(ctx, tag + "d_loaded")
                gu_hi = sem(ctx, tag + "gu_hi")
                gu_ready = sem(ctx, tag + "gu_ready")
                b_hi_s = sem(ctx, tag + "b_hi_s")
                b_ready = sem(ctx, tag + "b_ready")
                mix_mm = sem(ctx, tag + "mix_mm")
                down_s_ = sem(ctx, tag + "down_scaled")
                d_hi_s = sem(ctx, tag + "d_hi_s")
                d_ready = sem(ctx, tag + "d_ready")
                up_mm = sem(ctx, tag + "up_mm")
                silu_s = sem(ctx, tag + "silu_s")
                hid_s = sem(ctx, tag + "hid_s")
                hh_s = sem(ctx, tag + "hh_s")
                hl_s = sem(ctx, tag + "hl_s")
                down_mm = sem(ctx, tag + "down_mm")
                x_added = sem(ctx, tag + "x_added")
                chunks_before = [2 * s for s in range(len(segs))]

                with nc.Block() as block:
                    @block.sync
                    def _(sp):
                        if mixed:
                            pass
                        else:
                            sp.dma_start(gs[:], gate_s).then_inc(scales_loaded, 16)
                            sp.dma_start(us[:], up_s).then_inc(scales_loaded, 16)
                            sp.dma_start(drow, down_s.broadcast_to([P, D])).then_inc(scales_loaded, 16)
                        for s, seg in enumerate(segs):
                            w = len(seg) * P
                            c = slice(seg[0] * P, seg[0] * P + w)
                            if s:
                                sp.wait_ge(gu_ready, 2 * s)
                            sp.dma_start(raw_g[:, :, 0:w], tile_rows(gate_w)[:, :, c]).then_inc(gu_loaded, 16)
                            sp.dma_start(raw_u[:, :, 0:w], tile_rows(up_w)[:, :, c]).then_inc(gu_loaded, 16)
                            if s:
                                if mixed:
                                    sp.wait_ge(b_ready, s)
                                else:
                                    sp.wait_ge(down_s_, chunks_before[s])
                            sp.dma_start(raw_d[:, 0:len(seg), :], tile_rows(down_w[c, :])).then_inc(d_loaded, 16)
                        if store is not None:
                            last = len(steps) - NB
                            for b in range(NB):
                                for t in range(TB):
                                    sp.wait_ge(x_added, TB * (last + b) + t + 1)
                                    sp.dma_start(store[(TB * b + t) * P:(TB * b + t + 1) * P, :],
                                                 x[:, TB * b + t, :]).then_inc(stored, 16)
                            sp.wait_ge(stored, 16 * T)

                    @block.tensor
                    def _(pe):
                        def mix(s):
                            pe.wait_ge(b_ready, s + 1)
                            for c in range(len(segs[s])):
                                n = chunks_before[s] + c
                                if n:
                                    pe.wait_ge(down_s_, n)
                                nc.tensor.matmul(bank[7][:], hadamard[:], dh[:, s % 2, c, :], start=True, stop=False)
                                nc.tensor.matmul(bank[7][:], hadamard[:], dl[:, s % 2, c, :], start=False,
                                                 stop=True).then_inc(mix_mm, 1)

                        def up(k):
                            s, b = steps[k]
                            cols = slice(512 * b, 512 * b + 512)
                            if b == 0:
                                pe.wait_ge(gu_ready, 2 * (s + 1))
                            for c in range(len(segs[s])):
                                u = ubase[k] + c
                                if u >= 2:
                                    pe.wait_ge(hid_s, u - 1)
                                wc = slice(P * c, P * c + P)
                                for m in range(2):
                                    mm = product(bank[2 * (u % 2) + m][:],
                                                 lambda i: (wh[m][:, s % 2, i, wc], wl[m][:, s % 2, i, wc]),
                                                 lambda i: (ht[0][:, i, cols], ht[1][:, i, cols]), KT)
                                mm.then_inc(up_mm, 1)

                        def down_(k):
                            s, b = steps[k]
                            pe.wait_ge(d_ready, chunks_before[s] + len(segs[s]))
                            pe.wait_ge(hl_s, ubase[k + 1])
                            for t in range(TB):
                                n = TB * k + t
                                if n >= 3:
                                    pe.wait_ge(x_added, n - 2)
                                tc = slice(P * t, P * t + P)
                                product(bank[4 + n % 3][:],
                                        lambda i: (hh[:, k % 2, i, tc], hl[:, k % 2, i, tc]),
                                        lambda i: (dh[:, s % 2, i, :], dl[:, s % 2, i, :]),
                                        len(segs[s])).then_inc(down_mm, 1)

                        if mixed:
                            mix(0)
                        for k, (s, b) in enumerate(steps):
                            up(k)
                            if k:
                                down_(k - 1)
                            if mixed and b == 2 and s + 1 < len(segs):
                                mix(s + 1)
                        down_(len(steps) - 1)

                    @block.scalar
                    def _(act):
                        def weights(s):
                            w = len(segs[s]) * P
                            act.wait_ge(gu_loaded, 32 * (s + 1))
                            if s >= 2:
                                act.wait_ge(up_mm, ubase[NB * (s - 1)])
                            for m, raw in enumerate((raw_g, raw_u)):
                                nc.scalar.copy(wh[m][:, s % 2, :, 0:w], raw[:, :, 0:w]).then_inc(gu_hi, 1)
                            if mixed:
                                act.wait_ge(d_loaded, 16 * (s + 1))
                                if s >= 2:
                                    act.wait_ge(down_mm, TB * NB * (s - 1))
                                nc.scalar.copy(dh[:, s % 2, :, :], raw_d).then_inc(b_hi_s, 1)

                        def hidden_hi(k, c):
                            u = ubase[k] + c
                            act.wait_ge(hid_s, u + 1)
                            if k >= 2:
                                act.wait_ge(down_mm, TB * (k - 1))
                            nc.scalar.copy(hh[:, k % 2, c, :], act_[:, u % 2, :]).then_inc(hh_s, 1)

                        weights(0)
                        if not mixed:
                            act.wait_ge(scales_loaded, 48)
                        late = None
                        for k, (s, b) in enumerate(steps):
                            if b == 1 and s + 1 < len(segs):
                                weights(s + 1)
                            for c, ch in enumerate(segs[s]):
                                u = ubase[k] + c
                                act.wait_ge(up_mm, u + 1)
                                if u >= 2:
                                    act.wait_ge(hid_s, u - 1)
                                nc.scalar.activation(silu[:, u % 2, :], bank[2 * (u % 2)][:], ACT.Silu,
                                                     scale=1.0 if mixed else gs[:, ch:ch + 1]).then_inc(silu_s, 1)
                                if late:
                                    hidden_hi(*late)
                                late = (k, c)
                        hidden_hi(*late)

                    @block.vector
                    def _(dve):
                        if mixed:
                            nc.vector.tensor_scalar(drow, gate_rows[:, layer, 1, :], float(H0) ** -0.5, None,
                                                    ALU.mult).then_inc(drow_ready, 1)
                        else:
                            dve.wait_ge(scales_loaded, 48)
                            nc.vector.tensor_tensor(drow, drow, gate_rows[:, layer, 1, :],
                                                    ALU.mult).then_inc(drow_ready, 1)
                        dve.wait_ge(drow_ready, 1)

                        def weights(s):
                            w = len(segs[s]) * P
                            for m, raw in enumerate((raw_g, raw_u)):
                                dve.wait_ge(gu_hi, 2 * s + m + 1)
                                nc.vector.tensor_tensor(wl[m][:, s % 2, :, 0:w], raw[:, :, 0:w],
                                                        wh[m][:, s % 2, :, 0:w], ALU.subtract).then_inc(gu_ready, 1)
                            if mixed:
                                dve.wait_ge(b_hi_s, s + 1)
                                nc.vector.tensor_tensor(dl[:, s % 2, :, :], raw_d, dh[:, s % 2, :, :], ALU.subtract).then_inc(b_ready, 1)
                            else:
                                dve.wait_ge(d_loaded, 16 * (s + 1))

                        def down_weights(s):
                            if s >= 2:
                                dve.wait_ge(down_mm, TB * NB * (s - 1))
                            for c in range(len(segs[s])):
                                n = chunks_before[s] + c
                                if mixed:
                                    dve.wait_ge(mix_mm, n + 1)
                                src = bank[7][:] if mixed else raw_d[:, c, :]
                                nc.vector.tensor_tensor(down[:, c, :], src, drow, ALU.mult).then_inc(down_s_, 1)
                                dve.wait_ge(down_s_, n + 1)
                                nc.vector.tensor_copy(dh[:, s % 2, c, :], down[:, c, :]).then_inc(d_hi_s, 1)
                                dve.wait_ge(d_hi_s, n + 1)
                                nc.vector.tensor_tensor(dl[:, s % 2, c, :], down[:, c, :], dh[:, s % 2, c, :],
                                                        ALU.subtract).then_inc(d_ready, 1)

                        def hidden_lo(k, c):
                            u = ubase[k] + c
                            dve.wait_ge(hh_s, u + 1)
                            nc.vector.tensor_tensor(hl[:, k % 2, c, :], act_[:, u % 2, :], hh[:, k % 2, c, :],
                                                    ALU.subtract).then_inc(hl_s, 1)

                        def add_x(k):
                            s, b = steps[k]
                            for t in range(TB):
                                n = TB * k + t
                                dve.wait_ge(down_mm, n + 1)
                                if s:
                                    dve.wait_ge(x_added, n - TB * NB + 1)
                                xt = x[:, TB * b + t, :]
                                nc.vector.tensor_tensor(xt, bank[4 + n % 3][:], xt, ALU.add).then_inc(x_added, 1)

                        weights(0)
                        down_weights(0)
                        late = None
                        for k, (s, b) in enumerate(steps):
                            if b == 1 and s + 1 < len(segs):
                                weights(s + 1)
                            if b == 3 and s + 1 < len(segs):
                                down_weights(s + 1)
                            for c, ch in enumerate(segs[s]):
                                u = ubase[k] + c
                                dve.wait_ge(silu_s, u + 1)
                                if u >= 2:
                                    dve.wait_ge(hh_s, u - 1)
                                    dve.wait_ge(hl_s, u - 1)
                                up_bank = bank[2 * (u % 2) + 1][:]
                                if mixed:
                                    nc.vector.tensor_tensor(act_[:, u % 2, :], up_bank, silu[:, u % 2, :],
                                                            ALU.mult).then_inc(hid_s, 1)
                                else:
                                    nc.vector.scalar_tensor_tensor(out=act_[:, u % 2, :], in0=up_bank,
                                                                   scalar=us[:, ch:ch + 1], in1=silu[:, u % 2, :],
                                                                   op0=ALU.mult, op1=ALU.mult).then_inc(hid_s, 1)
                                if late:
                                    hidden_lo(*late)
                                late = (k, c)
                            if k:
                                add_x(k - 1)
                        hidden_lo(*late)
                        add_x(len(steps) - 1)

        with ExitStack() as ffn:
            h2_hi = sb(ffn, "h2_hi", [P, KT, S], F32R)
            h2_lo = sb(ffn, "h2_lo", [P, KT, S], F32R)
            with ExitStack() as ctx:
                res_loaded = [sem(ctx, f"res_loaded{b}") for b in range(NB)]
                out_p = project_out(ctx, "o0_", a["w_out0"], a["b_out0"], gate_rows[:, 0, 0, :],
                                    lambda b, g: ctx0[:, g, 512 * b:512 * b + 512],
                                    lambda act, b, g: None,
                                    lambda pool, t: pool.wait_ge(res_loaded[t // TB], 16), bufs=1)
                norm = Norm(ctx, "n2_", lambda b, t: x[:, TB * b + t, :], mod_cols[:, 0, SB, :],
                            mod_cols[:, 0, CB, :], h2_hi, h2_lo, zbufs=1)
                with nc.Block() as block:
                    @block.sync
                    def _(sp):
                        out_p.sync(sp)
                        for b in range(NB):
                            rows = slice(TB * b, TB * b + TB)
                            sp.dma_start(x[:, rows, :], tile_rows(a["L0_attn_x"])[:, rows, :]).then_inc(res_loaded[b], 16)

                    @block.gpsimd
                    def _(pool):
                        out_p.bias_gpsimd(pool)

                    @block.tensor
                    def _(pe):
                        for b in range(NB):
                            out_p.tensor(pe, b)
                            if b:
                                norm.tensor(pe, b - 1)
                        norm.tensor(pe, NB - 1)

                    @block.scalar
                    def _(act):
                        for b in range(NB):
                            out_p.hi_scalar(act, b)
                            if b:
                                norm.std_scalar(act, b - 1)
                                norm.h_scalar(act, b - 1)
                        norm.std_scalar(act, NB - 1)
                        norm.h_scalar(act, NB - 1)

                    @block.vector
                    def _(dve):
                        def normalise(b):
                            dve.wait_ge(out_p.ready, TB * (b + 1))
                            norm.stats_vector(dve, b)
                            norm.z_vector(dve, b)
                            norm.split_vector(dve, b)
                        out_p.weights_vector(dve)
                        for b in range(NB):
                            out_p.lo_vector(dve, b)
                            if b:
                                normalise(b - 1)
                            out_p.add_vector(dve, b)
                        normalise(NB - 1)

            feed_forward("f0_", 0, a["w1t"], a["w3t"], w2_mixed, H0, (h2_hi, h2_lo))

        with ExitStack() as ffn:
            qt = tokens_b[:, :].rearrange("p (g t) -> p g t", g=G)
            kv_cols = P + 2
            kv = sb(ffn, "kv", [P, G, P])
            k_sum = sb(ffn, "k_sum", [P, G, 32])
            if True:
                with ExitStack() as ctx:
                    ht_hi = sb(ctx, "ht5_hi", [P, KT, 2 * 512], F32R)
                    ht_lo = sb(ctx, "ht5_lo", [P, KT, 2 * 512], F32R)
                    w_hi = sb(ctx, "w5_hi", [P, 3, KT, D], F32R)
                    w_lo = sb(ctx, "w5_lo", [P, 3, KT, D], F32R)
                    w_raw = sb(ctx, "w5_raw", [P, KT, D])
                    bq = sb(ctx, "bq", [P, KT])
                    bk = sb(ctx, "bk", [P, D])
                    bv = sb(ctx, "bv", [P, D])
                    decay_row = sb(ctx, "decay_row", [P, 512])
                    decay_col = sb(ctx, "decay_col", [P, T])
                    bd_mask = sb(ctx, "bd_mask", [P, P])
                    head_mask = sb(ctx, "head_mask", [P, G, 32])
                    q_relu = sb(ctx, "q_relu", [P, 2, 512])
                    k_biased = sb(ctx, "k_biased", [P, 2, D])
                    k_tile = sb(ctx, "k_tile", [P, 2, D])
                    v_tile = sb(ctx, "v_tile", [P, 2, G, kv_cols])
                    w_loaded = sem(ctx, "w5_loaded")
                    w_hi_ready = sem(ctx, "w5_hi_s")
                    w_ready = sem(ctx, "w5_ready")
                    small_loaded = sem(ctx, "small_loaded")
                    decay_loaded = [sem(ctx, f"decay_loaded{b}") for b in range(NB)]
                    proj5 = sem(ctx, "proj5")
                    q_relued = sem(ctx, "q_relued")
                    read5 = sem(ctx, "read5")
                    k_ready = sem(ctx, "k_ready")
                    kv_mm = sem(ctx, "kv_mm")
                    ones_ready = sem(ctx, "ones5_ready")
                    norm = Norm(ctx, "n3_", lambda b, t: x[:, TB * b + t, :], mod_cols[:, 1, SA, :],
                                mod_cols[:, 1, CA, :], ht_hi, ht_lo,
                                used=lambda dve, b: dve.wait_ge(proj5, (G + 2 * TB) * (b - 1)), zbufs=1)
                    PER = G + 2 * TB
                    with nc.Block() as block:
                        @block.sync
                        def _(sp):
                            sp.dma_start(w_raw[:], tile_rows(a["w_qkv1"][0])).then_inc(w_loaded, 16)
                            sp.dma_start(bq[:], a["bq"]).then_inc(small_loaded, 16)
                            sp.dma_start(bk[:], a["bk"].broadcast_to([P, D])).then_inc(small_loaded, 16)
                            sp.dma_start(bv[:], a["bv"].broadcast_to([P, D])).then_inc(small_loaded, 16)
                            sp.dma_start(decay_col[:], a["decay_col"]).then_inc(small_loaded, 16)
                            sp.dma_start(bd_mask[:], a["const"][:, 6 * P:7 * P]).then_inc(small_loaded, 16)
                            sp.dma_start(head_mask[:], a["const"][:, 7 * P:8 * P].rearrange("p (g e) -> p g e", g=G)).then_inc(small_loaded, 16)
                            for i in range(1, 3):
                                sp.wait_ge(w_ready, i)
                                sp.dma_start(w_raw[:], tile_rows(a["w_qkv1"][i])).then_inc(w_loaded, 16)
                            for b in range(NB):
                                if b:
                                    sp.wait_ge(read5, PER * (b - 1) + G)
                                sp.dma_start(decay_row[:], a["decay_row"][:, 512 * b:512 * b + 512].broadcast_to([P, 512])).then_inc(decay_loaded[b], 16)

                        @block.tensor
                        def _(pe):
                            def kv_step(i):
                                pe.wait_ge(k_ready, i + 1)
                                pe.wait_ge(read5, PER * (i // TB) + G + 2 * (i % TB) + 2)
                                for g in range(G):
                                    first = i == 0 and g % 2 == 0
                                    mm = nc.tensor.matmul(bank[6 + g // 2][:, (g % 2) * kv_cols:(g % 2 + 1) * kv_cols],
                                                          k_tile[:, i % 2, P * g:P * g + P], v_tile[:, i % 2, g, :],
                                                          start=first, stop=(i == T - 1), skip_group_check=True)
                                mm.then_inc(kv_mm, 1)

                            def qkv(b):
                                pe.wait_ge(norm.ht_ready, KT * (b + 1))
                                cols = norm.cols(b)
                                for m in range(PER):
                                    n = PER * b + m
                                    if n >= 4:
                                        pe.wait_ge(read5, n - 3)
                                    dst = bank[2 + n % 4][:]
                                    if m < G:
                                        if n == 0:
                                            pe.wait_ge(w_ready, 1)
                                        c = slice(P * m, P * m + P)
                                        mm = product(dst, lambda k: (w_hi[:, 0, k, c], w_lo[:, 0, k, c]),
                                                     lambda k: (ht_hi[:, k, cols], ht_lo[:, k, cols]), KT)
                                    else:
                                        if b == 0:
                                            pe.wait_ge(w_ready, 3)
                                        i = 1 + (m - G) % 2
                                        at = cols.start + P * ((m - G) // 2)
                                        c = slice(at, at + P)
                                        mm = product(dst, lambda k: (ht_hi[:, k, c], ht_lo[:, k, c]),
                                                     lambda k: (w_hi[:, i, k, :], w_lo[:, i, k, :]), KT)
                                    mm.then_inc(proj5, 1)
                                    if m >= G and (m - G) % 2 == 0 and TB * b + (m - G) // 2 >= 1:
                                        kv_step(TB * b + (m - G) // 2 - 1)
                            pe.wait_ge(ones_ready, 1)
                            norm.tensor(pe, 0)
                            for b in range(NB):
                                if b + 1 < NB:
                                    norm.tensor(pe, b + 1)
                                qkv(b)
                            kv_step(T - 1)

                        @block.scalar
                        def _(act):
                            def weights(i):
                                act.wait_ge(w_loaded, 16 * (i + 1))
                                nc.scalar.copy(w_hi[:, i, :, :], w_raw[:]).then_inc(w_hi_ready, 1)

                            def relus(b):
                                for m in range(G):
                                    n, e = PER * b + m, G * b + m
                                    act.wait_ge(proj5, n + 1)
                                    if e >= 2:
                                        act.wait_ge(read5, PER * ((e - 2) // G) + (e - 2) % G + 1)
                                    nc.scalar.activation(q_relu[:, e % 2, :], bank[2 + n % 4][:], ACT.Relu,
                                                         bias=bq[:, m:m + 1]).then_inc(q_relued, 1)
                                for t in range(TB):
                                    i = TB * b + t
                                    act.wait_ge(read5, PER * b + G + 2 * t + 1)
                                    if i >= 2:
                                        act.wait_ge(kv_mm, i - 1)
                                    nc.scalar.activation(k_tile[:, i % 2, :], k_biased[:, i % 2, :], ACT.Relu,
                                                         scale=decay_col[:, i:i + 1]).then_inc(k_ready, 1)
                            norm.std_scalar(act, 0)
                            weights(0)
                            norm.h_scalar(act, 0)
                            weights(1)
                            norm.std_scalar(act, 1)
                            weights(2)
                            act.wait_ge(small_loaded, 96)
                            for b in range(NB):
                                if b + 1 < NB:
                                    norm.h_scalar(act, b + 1)
                                if b + 2 < NB:
                                    norm.std_scalar(act, b + 2)
                                relus(b)

                        @block.vector
                        def _(dve):
                            def weights(i):
                                dve.wait_ge(w_hi_ready, i + 1)
                                nc.vector.tensor_tensor(w_lo[:, i, :, :], w_raw[:], w_hi[:, i, :, :],
                                                        ALU.subtract).then_inc(w_ready, 1)

                            def rest(b):
                                dve.wait_ge(decay_loaded[b], 16)
                                for m in range(G):
                                    e = G * b + m
                                    dve.wait_ge(q_relued, e + 1)
                                    nc.vector.tensor_tensor(qt[:, m, 512 * b:512 * b + 512], q_relu[:, e % 2, :],
                                                            decay_row[:], ALU.mult).then_inc(read5, 1)
                                for t in range(TB):
                                    i, n = TB * b + t, PER * b + G + 2 * t
                                    dve.wait_ge(proj5, n + 1)
                                    if i >= 2:
                                        dve.wait_ge(k_ready, i - 1)
                                    nc.vector.tensor_tensor(k_biased[:, i % 2, :], bank[2 + n % 4][:], bk[:],
                                                            ALU.add).then_inc(read5, 1)
                                    dve.wait_ge(proj5, n + 2)
                                    if i >= 2:
                                        dve.wait_ge(kv_mm, i - 1)
                                    nc.vector.tensor_tensor(v_tile[:, i % 2, :, 0:P],
                                                            bank[2 + (n + 1) % 4][:].rearrange("p (g e) -> p g e", g=G),
                                                            bv[:].rearrange("p (g e) -> p g e", g=G),
                                                            ALU.add).then_inc(read5, 1)
                            nc.vector.memset(v_tile[:, :, :, P:kv_cols], 1.0).then_inc(ones_ready, 1)
                            norm.stats_vector(dve, 0)
                            norm.z_vector(dve, 0)
                            weights(0)
                            norm.stats_vector(dve, 1)
                            norm.split_vector(dve, 0)
                            norm.z_vector(dve, 1)
                            weights(1)
                            weights(2)
                            dve.wait_ge(small_loaded, 96)
                            for b in range(NB):
                                if b + 1 < NB:
                                    norm.split_vector(dve, b + 1)
                                if b + 2 < NB:
                                    norm.stats_vector(dve, b + 2)
                                    norm.z_vector(dve, b + 2)
                                rest(b)
                            dve.wait_ge(kv_mm, T)
                            for g in range(G):
                                src = bank[6 + g // 2][:, (g % 2) * kv_cols:(g % 2 + 1) * kv_cols]
                                nc.vector.tensor_tensor(kv[:, g, :], src[:, 0:P], bd_mask[:], ALU.mult)
                                nc.vector.tensor_scalar(k_sum[:, g, :], head_mask[:, g, :], src[:, P:P + 1], None, ALU.mult)

                h2_hi = sb(ffn, "h3_hi", [P, KT, S], F32R)
                h2_lo = sb(ffn, "h3_lo", [P, KT, S], F32R)
                with ExitStack() as ctx:
                    z_sum = sb(ctx, "z_sum", [P, 512])
                    zb = sb(ctx, "zb", [P, G, 512])
                    at = qt
                    den_mm = sem(ctx, "den_mm")
                    z_step = sem(ctx, "z_step")
                    z_stored = sem(ctx, "z_stored")
                    z_loaded = [sem(ctx, f"z_loaded{b}") for b in range(NB)]
                    num_mm = sem(ctx, "num_mm")
                    at_ready = sem(ctx, "at_ready")
                    out_p = project_out(ctx, "o1_", a["w_out1"], a["b_out1"], gate_rows[:, 1, 0, :],
                                        lambda b, g: at[:, g, 512 * b:512 * b + 512],
                                        lambda act, b, g: act.wait_ge(at_ready, G * b + g + 1),
                                        lambda pool, t: None, bufs=1)
                    norm = Norm(ctx, "n4_", lambda b, t: x[:, TB * b + t, :], mod_cols[:, 1, SB, :],
                                mod_cols[:, 1, CB, :], h2_hi, h2_lo, zbufs=1)
                    with nc.Block() as block:
                        @block.sync
                        def _(sp):
                            out_p.sync(sp)
                            sp.wait_ge(z_step, 2)
                            sp.dma_start(z_dram[:, :], z_sum[:]).then_inc(z_stored, 16)
                            sp.wait_ge(z_stored, 16)
                            for b in range(NB):
                                if b:
                                    sp.wait_ge(at_ready, G * b)
                                for h in range(HEADS):
                                    g, r = h // 4, 32 * (h % 4)
                                    sp.dma_start(zb[r:r + 32, g, :],
                                                 z_dram[32 * b + h:32 * b + h + 1, :].broadcast_to([32, 512])).then_inc(z_loaded[b], 16)

                        @block.gpsimd
                        def _(pool):
                            out_p.bias_gpsimd(pool)

                        @block.tensor
                        def _(pe):
                            for g in range(G):
                                for b in range(NB):
                                    last = nc.tensor.matmul(bank[7][32 * b:32 * b + 32, :], k_sum[:, g, :],
                                                            qt[:, g, 512 * b:512 * b + 512],
                                                            start=(g == 0), stop=(g == G - 1))
                            last.then_inc(den_mm, 1)

                            def numerators(b):
                                for g in range(G):
                                    i = G * b + g
                                    if i >= 1:
                                        pe.wait_ge(at_ready, i)
                                    nc.tensor.matmul(bank[6][:], kv[:, g, :], qt[:, g, 512 * b:512 * b + 512],
                                                     start=True, stop=True).then_inc(num_mm, 1)
                            numerators(0)
                            for b in range(NB):
                                if b + 1 < NB:
                                    numerators(b + 1)
                                out_p.tensor(pe, b)
                                if b:
                                    norm.tensor(pe, b - 1)
                            norm.tensor(pe, NB - 1)

                        @block.scalar
                        def _(act):
                            for b in range(NB):
                                out_p.hi_scalar(act, b)
                                if b:
                                    norm.std_scalar(act, b - 1)
                                    norm.h_scalar(act, b - 1)
                            norm.std_scalar(act, NB - 1)
                            norm.h_scalar(act, NB - 1)

                        @block.vector
                        def _(dve):
                            dve.wait_ge(den_mm, 1)
                            nc.vector.tensor_scalar(z_sum[:], bank[7][:], Z_EPS, None, ALU.add).then_inc(z_step, 1)
                            dve.wait_ge(z_step, 1)
                            nc.vector.reciprocal(z_sum[:], z_sum[:]).then_inc(z_step, 1)
                            out_p.weights_vector(dve)

                            def attended(b):
                                dve.wait_ge(z_loaded[b], 16 * HEADS)
                                for g in range(G):
                                    i = G * b + g
                                    dve.wait_ge(num_mm, i + 1)
                                    nc.vector.tensor_tensor(at[:, g, 512 * b:512 * b + 512], bank[6][:], zb[:, g, :],
                                                            ALU.mult).then_inc(at_ready, 1)

                            def normalise(b):
                                dve.wait_ge(out_p.ready, TB * (b + 1))
                                norm.stats_vector(dve, b)
                                norm.z_vector(dve, b)
                                norm.split_vector(dve, b)
                            attended(0)
                            for b in range(NB):
                                out_p.lo_vector(dve, b)
                                if b + 1 < NB:
                                    attended(b + 1)
                                if b:
                                    normalise(b - 1)
                                out_p.add_vector(dve, b)
                            normalise(NB - 1)

            feed_forward("f1_", 1, a["gate_wt"], a["up_wt"], a["down_wt"], H1, (h2_hi, h2_lo),
                         a["gate_s"], a["up_s"], a["down_s"], store=out)


def _constants():
    import numpy as np

    i = np.arange(P)
    eye = np.eye(P, dtype=np.float32)
    signs = np.array([[1.0]], np.float32)
    while signs.shape[0] < P:
        signs = np.block([[signs, signs], [signs, -signs]])
    full = np.full((P, P), MASKED, np.float32)
    later_key = np.where(i[:, None] > i[None, :], np.float32(MASKED), np.float32(0))
    by_key = np.concatenate([full, later_key], 1)
    by_query = np.concatenate([later_key.T, full], 1)
    same_head = (i[:, None] // HD == i[None, :] // HD).astype(np.float32)
    column = np.zeros((P, G, 32), np.float32)
    for g in range(G):
        column[i, g, 4 * g + i // HD] = 1.0
    const = np.concatenate([eye, signs, by_key, by_query, same_head, column.reshape(P, -1)], 1)
    decay = np.exp(-np.arange(S, dtype=np.float32) / np.float32(S)).astype(np.float32)
    return const.astype(np.float32), decay


def kernel(**inputs):
    import numpy as np
    import concourse.bacc as bacc
    from concourse.bass_utils import run_bass_kernel_spmd

    const, decay = _constants()
    w = np.asarray(inputs["L0_attn_W_qkv"]).reshape(D, HEADS, 3, HD)
    b = np.asarray(inputs["L0_attn_b_qkv"]).reshape(HEADS, 3, HD)
    flat = lambda m: np.asarray(m).reshape(-1, P).T
    row = lambda m: np.asarray(m).reshape(1, -1)
    arrays = {
        "L0_attn_x": np.asarray(inputs["L0_attn_x"])[0],
        "w_qkv": w.transpose(2, 0, 1, 3).reshape(3, D, D),
        "qk_bias": np.concatenate([flat(b[:, 0]), flat(b[:, 1])], 1),
        "v_bias": row(b[:, 2]),
        "w_out0": inputs["L0_attn_W_out"], "b_out0": row(inputs["L0_attn_b_out"]),
        "w1t": np.asarray(inputs["L0_ffn_W1"]).T, "w3t": np.asarray(inputs["L0_ffn_W3"]).T,
        "w2t": np.asarray(inputs["L0_ffn_W2"]).T,
        "L0_c": flat(inputs["L0_c"]), "L0_wmod": inputs["L0_wmod"], "L1_c": flat(inputs["L1_c"]), "L1_wmod": inputs["L1_wmod"],
        "w_qkv1": np.stack([np.asarray(inputs[f"L1_attn_W{n}"]).T for n in "qkv"]),
        "bq": flat(inputs["L1_attn_bq"]), "bk": row(inputs["L1_attn_bk"]), "bv": row(inputs["L1_attn_bv"]),
        "w_out1": np.asarray(inputs["L1_attn_Wo"]).T, "b_out1": row(inputs["L1_attn_bo"]),
        "gate_wt": np.asarray(inputs["L1_ffn_gate_w"]).T, "up_wt": np.asarray(inputs["L1_ffn_up_w"]).T,
        "down_wt": np.asarray(inputs["L1_ffn_down_w"]).T,
        "gate_s": flat(inputs["L1_ffn_gate_s"]), "up_s": flat(inputs["L1_ffn_up_s"]),
        "down_s": row(inputs["L1_ffn_down_s"]),
        "const": const, "decay_row": decay.reshape(1, S), "decay_col": decay.reshape(T, P).T,
    }
    nc = bacc.Bacc("TRN2", target_bir_lowering=False, num_devices=1)
    fed, aps = {}, {}
    for name, m in arrays.items():
        m = np.ascontiguousarray(m)
        fed[f"in_{name}"] = m
        aps[name] = nc.dram_tensor(f"in_{name}", m.shape, mybir.dt.from_np(m.dtype), kind="ExternalInput").ap()
    out = nc.dram_tensor("out", (S, D), F32, kind="ExternalOutput").ap()
    build_program(nc, aps, out)
    r = run_bass_kernel_spmd(nc, [fed], core_ids=[0])
    return r.results[0]["out"].reshape(1, S, D)
```

```python
from contextlib import ExitStack

import concourse.bass as bass
from concourse import mybir

F32 = mybir.dt.float32
F32R = mybir.dt.float32r
BF16 = mybir.dt.bfloat16
ALU = mybir.AluOpType
ACT = mybir.ActivationFunctionType
AX_X = mybir.AxisListType.X

P = 128
S = 2048
D = 512
HEADS = 16
HD = D // HEADS
G = HEADS // 4
KT = D // P
T = S // P
NB = S // 512
TB = 512 // P
H0 = 2048
H1 = 1408
LN_EPS = 1e-5
Z_EPS = 1e-6
SCALE = float(HD) ** -0.5
MASKED = -32768.0
BIASROW = 3 * HD


def build_program(nc, a, out):
    with ExitStack() as whole:
        def sb(ctx, name, shape, dt=F32):
            return ctx.enter_context(nc.sbuf_tensor(name, shape, dt))

        held = {}

        def sem(ctx, name):
            def give_back():
                nc.clear_and_free_semaphores(held.pop(id(ctx)))
                nc.all_engine_barrier()
            if id(ctx) not in held:
                held[id(ctx)] = []
                if ctx is not whole:
                    ctx.callback(give_back)
            held[id(ctx)].append(nc.alloc_semaphore(name))
            return held[id(ctx)][-1]

        def dram(name, shape, dt=F32):
            return nc.dram_tensor(name, shape, dt).ap()

        stored = sem(whole, "output_stored")
        banks = whole.enter_context(nc.psum_tensor("banks", [P, 8, 512], F32))
        bank = [banks[:, i, :] for i in range(8)]

        ident = sb(whole, "ident", [P, P])
        ident16 = sb(whole, "ident16", [P, P], BF16)
        mask_keys = sb(whole, "mask_keys", [P, 2 * P], BF16)
        mask_queries = sb(whole, "mask_queries", [P, 2 * P], BF16)
        hadamard = sb(whole, "hadamard", [P, P], F32R)
        mod_cols = sb(whole, "mod_cols", [P, 2, 6, KT])
        tokens_a = sb(whole, "tokens_a", [P, T, D])
        tokens_b = sb(whole, "tokens_b", [P, T * D])
        early = sb(whole, "early_weights", [P, KT * D])
        early_loaded = sem(whole, "early_loaded")
        early_square = early[:].rearrange("p (k d) -> p k d", k=KT)
        early_pair = early[:].rearrange("p (m k d) -> p m k d", m=2, k=KT)
        early_gate = sb(whole, "early_gate", [P, D])
        OUT0, FFN0, QUERY1, OUT1, FFN1 = 32, 64, 80, 112, 144
        x = tokens_a
        SA, CA, GA, SB, CB, GB = range(6)

        q_hi, q_lo, k_hi, k_lo = (dram(n, [G, P, S]) for n in ("q_hi", "q_lo", "k_hi", "k_lo"))
        w2_mixed = dram("w2_mixed", [H0, D])
        gates = dram("gates", [2 * 2, D])
        max_dram = dram("max_dram", [2, 2 * 4 * TB, P])

        def tile_rows(ap):
            return ap.rearrange("(t p) d -> p t d", p=P)

        def load_early_projection(sp, w, layer):
            sp.dma_start(early_square, tile_rows(w)).then_inc(early_loaded, 16)
            sp.dma_start(early_gate[:], gates[2 * layer:2 * layer + 1, :].broadcast_to([P, D])).then_inc(early_loaded, 16)

        def load_early_pair(sp, gate_w, up_w):
            for m, w in enumerate((gate_w, up_w)):
                sp.dma_start(early_pair[:, m, :, :], tile_rows(w)[:, :, 0:2 * P]).then_inc(early_loaded, 16)

        class Norm:

            def __init__(self, ctx, tag, src, shift, scale, ht_hi, ht_lo, used=None, zbufs=2):
                self.used = used
                self.src, self.shift, self.scale, self.ht = src, shift, scale, (ht_hi, ht_lo)
                self.stats = sb(ctx, tag + "stats", [P, TB, 6])
                self.mv = sb(ctx, tag + "mv", [P, 2, TB, 2])
                self.ve = sb(ctx, tag + "ve", [P, 2, TB])
                self.std = sb(ctx, tag + "std", [P, 2, TB])
                self.rstd = sb(ctx, tag + "rstd", [P, 2, TB])
                self.zbufs = zbufs
                self.z = sb(ctx, tag + "z", [P, zbufs, TB, D])
                self.h = sb(ctx, tag + "h", [P, 2, 512])
                self.stats_done = sem(ctx, tag + "stats_done")
                self.std_done = sem(ctx, tag + "std_done")
                self.z_ready = sem(ctx, tag + "z_ready")
                self.turned = sem(ctx, tag + "turned")
                self.h_ready = sem(ctx, tag + "h_ready")
                self.hi_ready = sem(ctx, tag + "hi_ready")
                self.ht_ready = sem(ctx, tag + "ht_ready")

            def cols(self, b):
                at = 512 * (b % 2 if self.used else b)
                return slice(at, at + 512)

            def half_stats_vector(self, dve, b, half):
                for t in (2 * half, 2 * half + 1):
                    nc.vector.bn_stats(self.stats[:, t, :], self.src(b, t)).then_inc(self.stats_done, 1)

            def stats_vector(self, dve, b, halves=(0, 1)):
                q, base = b % 2, 10 * b
                for half in halves:
                    self.half_stats_vector(dve, b, half)
                for t in range(TB):
                    dve.wait_ge(self.stats_done, base + t + 1)
                    nc.vector.bn_aggr(self.mv[:, q, t, :], self.stats[:, t, :]).then_inc(self.stats_done, 1)
                dve.wait_ge(self.stats_done, base + 8)
                nc.vector.tensor_scalar(self.ve[:, q, :], self.mv[:, q, :, 1], LN_EPS, None,
                                        ALU.add).then_inc(self.stats_done, 1)

            def std_scalar(self, act, b):
                q = b % 2
                act.wait_ge(self.stats_done, 10 * b + 9)
                nc.scalar.activation(self.std[:, q, :], self.ve[:, q, :], ACT.Sqrt).then_inc(self.std_done, 1)

            def z_vector(self, dve, b):
                q = b % 2
                dve.wait_ge(self.std_done, b + 1)
                nc.vector.reciprocal(self.rstd[:, q, :], self.std[:, q, :]).then_inc(self.stats_done, 1)
                dve.wait_ge(self.stats_done, 10 * b + 10)
                if b >= self.zbufs:
                    dve.wait_ge(self.turned, KT * (b - self.zbufs + 1))
                for t in range(TB):
                    nc.vector.tensor_scalar(self.z[:, b % self.zbufs, t, :], self.src(b, t), self.mv[:, q, t, 0:1],
                                            self.rstd[:, q, t:t + 1], ALU.subtract,
                                            ALU.mult).then_inc(self.z_ready, 1)

            def tensor(self, pe, b):
                pe.wait_ge(self.z_ready, TB * (b + 1))
                for k in range(KT):
                    i = KT * b + k
                    if i >= 2:
                        pe.wait_ge(self.h_ready, i - 1)
                    for t in range(TB):
                        last = nc.tensor.transpose(bank[i % 2][:, t * P:(t + 1) * P],
                                                   self.z[:, b % self.zbufs, t, k * P:(k + 1) * P], ident[:])
                    last.then_inc(self.turned, 1)

            def h_scalar(self, act, b):
                def hi(k):
                    i = KT * b + k
                    if self.used and b >= 2 and k == 0:
                        self.used(act, b)
                    act.wait_ge(self.h_ready, i + 1)
                    nc.scalar.copy(self.ht[0][:, k, self.cols(b)], self.h[:, i % 2, :]).then_inc(self.hi_ready, 1)
                for k in range(KT):
                    i = KT * b + k
                    act.wait_ge(self.turned, i + 1)
                    if i >= 2:
                        act.wait_ge(self.ht_ready, i - 1)
                    nc.scalar.activation(self.h[:, i % 2, :], bank[i % 2][:], ACT.Identity,
                                         bias=self.shift[:, k:k + 1],
                                         scale=self.scale[:, k:k + 1]).then_inc(self.h_ready, 1)
                    if k % 2:
                        hi(k - 1)

            def split_vector(self, dve, b):
                for k in range(KT):
                    i, cols = KT * b + k, self.cols(b)
                    if k % 2:
                        dve.wait_ge(self.h_ready, i + 1)
                        nc.vector.tensor_copy(self.ht[0][:, k, cols], self.h[:, i % 2, :]).then_inc(self.hi_ready, 1)
                    dve.wait_ge(self.hi_ready, i + 1)
                    nc.vector.tensor_tensor(self.ht[1][:, k, cols], self.h[:, i % 2, :],
                                            self.ht[0][:, k, cols], ALU.subtract).then_inc(self.ht_ready, 1)

        HALF = 6

        def product(dst, lhs, rhs, n, first=True, last=True, before=None):
            for i in range(n):
                if before:
                    before(i)
                lh, ll = lhs(i)
                rh, rl = rhs(i)
                nc.tensor.matmul(dst, lh, rh, start=(first and i == 0), stop=False)
                nc.tensor.matmul(dst, lh, rl, start=False, stop=False)
                mm = nc.tensor.matmul(dst, ll, rh, start=False, stop=(last and i == n - 1))
            return mm

        with ExitStack() as ctx:
            x0 = tokens_b[:, :].rearrange("p (t d) -> p t d", t=T)
            v = tokens_a
            w_raw = [v[:, TB * i:TB * i + TB, :] for i in range(2)] + [early_square]
            wmod = [v[:, TB * (2 + i):TB * (3 + i), :] for i in range(2)]
            ht_hi = sb(ctx, "ht_hi", [P, KT, 2 * 512], F32R)
            ht_lo = sb(ctx, "ht_lo", [P, KT, 2 * 512], F32R)
            w_hi = sb(ctx, "qkv_w_hi", [P, 3, KT, D], F32R)
            w_lo = sb(ctx, "qkv_w_lo", [P, 3, KT, D], F32R)
            bias_cols = sb(ctx, "qk_bias", [P, 2 * G])
            bias_v = sb(ctx, "v_bias", [P, D])
            out_hi = sb(ctx, "qk_out_hi", [P, 2, 512], F32R)
            out_lo = sb(ctx, "qk_out_lo", [P, 2, 512], F32R)
            stage = sb(ctx, "const_stage", [P, 6 * P])
            picks = sb(ctx, "picks", [P, P])
            ccol = sb(ctx, "ccol", [P, 2, KT])
            csilu = sb(ctx, "csilu", [P, 2, KT])
            cwide = sb(ctx, "cwide", [P, 2, KT, 32])
            mod_parts = sb(ctx, "mod_parts", [P, 2, D])
            gate_rows = sb(ctx, "gate_rows", [P, 2, 2, D])
            gate_sign = sb(ctx, "gate_sign", [P, D])
            gate_size = sb(ctx, "gate_size", [P, D])
            x_loaded = [sem(ctx, f"x_loaded{b}") for b in range(NB)]
            w_loaded = [sem(ctx, f"w_loaded{i}") for i in range(3)]
            w_chunk_loaded = [sem(ctx, f"w_chunk_loaded{k}") for k in range(KT)]
            bias_loaded = sem(ctx, "bias_loaded")
            c_loaded = sem(ctx, "c_loaded")
            const_loaded = sem(ctx, "const_loaded")
            picks_loaded = sem(ctx, "picks_loaded")
            const_ready = sem(ctx, "const_ready")
            csilu_ready = sem(ctx, "csilu_ready")
            cwide_ready = sem(ctx, "cwide_ready")
            wmod_loaded = [sem(ctx, f"wmod_loaded{i}") for i in range(2)]
            mod_mm = sem(ctx, "mod_mm")
            mod_copied = sem(ctx, "mod_copied")
            mod_sum = sem(ctx, "mod_sum")
            mod_read = sem(ctx, "mod_read")
            gate_step = sem(ctx, "gate_step")
            gates_stored = sem(ctx, "gates_stored")
            w_hi_ready = sem(ctx, "w_hi_ready")
            w_ready = sem(ctx, "w_ready")
            qkv_done = sem(ctx, "qkv_done")
            qk_hi_ready = sem(ctx, "qk_hi_ready")
            qkv_out = sem(ctx, "qkv_out")
            qk_lo_ready = sem(ctx, "qk_lo_ready")
            qk_stored = [sem(ctx, f"qk_stored{i}") for i in range(2)]
            PER = 2 * G + TB
            norm = Norm(ctx, "n1_", lambda b, t: x0[:, TB * b + t, :], mod_cols[:, 0, SA, :],
                        mod_cols[:, 0, CA, :], ht_hi, ht_lo,
                        used=lambda act, b: act.wait_ge(qkv_done, PER * (b - 1)))
            VECTORS = [(l, vec) for l in range(2) for vec in (SA, CA, SB, CB, GA, GB)]

            def block_order(b, item, modulate, hooks):
                for m in range(PER):
                    item(b, m)
                    q = PER * b + m
                    if q < 2 * (len(VECTORS) - 2):
                        modulate(q)
                    if m in hooks and b + 1 < NB:
                        hooks[m](b + 1)

            with nc.Block() as block:
                @block.sync
                def _(sp):
                    xt = tile_rows(a["L0_attn_x"])

                    def load_mod(i):
                        l, vec = VECTORS[i]
                        if i >= 2:
                            sp.wait_ge(mod_mm, i - 1)
                        w = a[("L0_wmod", "L1_wmod")[l]][:, vec * D:(vec + 1) * D]
                        sp.dma_start(wmod[i % 2], tile_rows(w)).then_inc(wmod_loaded[i % 2], 16)

                    def load_x(b):
                        rows = slice(TB * b, TB * b + TB)
                        sp.dma_start(x0[:, rows, :], xt[:, rows, :]).then_inc(x_loaded[b], 16)
                    sp.dma_start(ccol[:, 0, :], a["L0_c"]).then_inc(c_loaded, 16)
                    sp.dma_start(ccol[:, 1, :], a["L1_c"]).then_inc(c_loaded, 16)
                    load_x(0)
                    load_mod(0)
                    load_mod(1)
                    sp.dma_start(stage[:], a["const"][:, 0:6 * P]).then_inc(const_loaded, 16)
                    sp.dma_start(picks[:], a["const"][:, 8 * P:9 * P]).then_inc(picks_loaded, 16)
                    for k in range(KT):
                        sp.dma_start(w_raw[0][:, k, :], tile_rows(a["w_qkv"][0])[:, k, :]).then_inc(w_chunk_loaded[k], 16)
                    sp.dma_start(bias_cols[:], a["qk_bias"]).then_inc(bias_loaded, 16)
                    sp.dma_start(bias_v[:], a["v_bias"].broadcast_to([P, D])).then_inc(bias_loaded, 16)
                    load_x(1)
                    sp.dma_start(w_raw[1], tile_rows(a["w_qkv"][1])).then_inc(w_loaded[1], 16)
                    sp.dma_start(w_raw[2], tile_rows(a["w_qkv"][2])).then_inc(w_loaded[2], 16)
                    load_x(2)
                    load_x(3)
                    for i in range(2, len(VECTORS)):
                        load_mod(i)

                @block.gpsimd
                def _(pool):
                    for e in range(NB * 2 * G):
                        b, m = e // (2 * G), e % (2 * G)
                        hi, lo = ((q_hi, q_lo), (k_hi, k_lo))[m // G]
                        cols = slice(512 * b, 512 * b + 512)
                        pool.wait_ge(qk_hi_ready, e + 1)
                        pool.dma_start(hi[m % G, :, cols], out_hi[:, e % 2, :].bitcast(F32)).then_inc(qk_stored[e % 2], 16)
                        pool.wait_ge(qk_lo_ready, e + 1)
                        pool.dma_start(lo[m % G, :, cols], out_lo[:, e % 2, :].bitcast(F32)).then_inc(qk_stored[e % 2], 16)
                    pool.wait_ge(gate_step, 4 * 4)
                    pool.dma_start(gates.rearrange("(one r) d -> one r d", one=1),
                                   gate_rows[0:1, :, :, :].rearrange("p l g d -> p (l g) d")).then_inc(gates_stored, 16)
                    pool.wait_ge(gates_stored, 16)
                    for i in range(2):
                        pool.wait_ge(qk_stored[i], 32 * NB * G)

                @block.tensor
                def _(pe):
                    def modulate(q):
                        i, second = 2 + q // 2, q % 2
                        (sums if second else products)(i)

                    def products(i):
                        l, vec = VECTORS[i]
                        pe.wait_ge(wmod_loaded[i % 2], 16 * (i // 2 + 1))
                        if i == 0:
                            pe.wait_ge(cwide_ready, 1)
                        else:
                            pe.wait_ge(mod_copied, i)
                        for k in range(KT):
                            mm = nc.tensor.matmul(bank[6][32 * k:32 * k + 32, :], cwide[:, l, k, :],
                                                  wmod[i % 2][:, k, :], start=True, stop=True)
                        mm.then_inc(mod_mm, 1)

                    def sums(i):
                        l, vec = VECTORS[i]
                        pe.wait_ge(mod_copied, i + 1)
                        if i == 0:
                            pe.wait_ge(picks_loaded, 16)
                        else:
                            pe.wait_ge(mod_read, i)
                        if vec in (GA, GB):
                            mm = nc.tensor.matmul(bank[7][:], picks[:], mod_parts[:, i % 2, :], start=True, stop=True)
                        else:
                            for k in range(KT):
                                mm = nc.tensor.matmul(bank[7][:, k:k + 1], mod_parts[:, i % 2, P * k:P * k + P],
                                                      picks[:, 0:1], start=True, stop=True)
                        mm.then_inc(mod_sum, 1)

                    def item(b, m):
                        cols = norm.cols(b)
                        n = PER * b + m
                        if b == 0 and m % G == 0 and m:
                            pe.wait_ge(w_ready, KT + m // G)

                        def chunk_ready(k):
                            pe.wait_ge(norm.ht_ready, KT * b + k + 1)
                            if b == 0:
                                pe.wait_ge(w_ready, k + 1)
                        if n >= 4:
                            pe.wait_ge(qkv_out, n - 3)
                        dst = bank[2 + n % 4][:]
                        if m < 2 * G:
                            i, c = m // G, slice(P * (m % G), P * (m % G) + P)
                            mm = product(dst, lambda k: (w_hi[:, i, k, c], w_lo[:, i, k, c]),
                                         lambda k: (ht_hi[:, k, cols], ht_lo[:, k, cols]), KT,
                                         before=chunk_ready if m == 0 else None)
                        else:
                            at = cols.start + P * (m - 2 * G)
                            c = slice(at, at + P)
                            mm = product(dst, lambda k: (ht_hi[:, k, c], ht_lo[:, k, c]),
                                         lambda k: (w_hi[:, 2, k, :], w_lo[:, 2, k, :]), KT)
                        mm.then_inc(qkv_done, 1)

                    for i in range(2):
                        products(i)
                        sums(i)
                    pe.wait_ge(const_ready, 1)
                    norm.tensor(pe, 0)
                    for b in range(NB):
                        block_order(b, item, modulate, {HALF - 1: lambda nb: norm.tensor(pe, nb)})

                @block.scalar
                def _(act):
                    def modulate(q):
                        i, second = 2 + q // 2, q % 2
                        if second == 0:
                            copy_parts(i)

                    def copy_parts(i):
                        act.wait_ge(mod_mm, i + 1)
                        if i >= 2:
                            act.wait_ge(mod_sum, i - 1)
                        nc.scalar.copy(mod_parts[:, i % 2, :], bank[6][:]).then_inc(mod_copied, 1)

                    def item(b, m):
                        if m >= 2 * G:
                            return
                        e = 2 * G * b + m
                        if e == 0:
                            act.wait_ge(bias_loaded, 32)
                        act.wait_ge(qkv_done, PER * b + m + 1)
                        if e >= 2:
                            act.wait_ge(qk_stored[e % 2], 32 * (e // 2))
                        nc.scalar.activation(out_hi[:, e % 2, :], bank[2 + (PER * b + m) % 4][:], ACT.Identity,
                                             bias=bias_cols[:, m:m + 1]).then_inc(qk_hi_ready, 1)

                    def weights(i):
                        if i == 0:
                            for k in range(KT):
                                act.wait_ge(w_chunk_loaded[k], 16)
                                nc.scalar.copy(w_hi[:, 0, k, :], w_raw[0][:, k, :]).then_inc(w_hi_ready, 1)
                            return
                        act.wait_ge(w_loaded[i], 16)
                        nc.scalar.copy(w_hi[:, i, :, :], w_raw[i]).then_inc(w_hi_ready, 1)
                    act.wait_ge(c_loaded, 32)
                    nc.scalar.activation(csilu[:], ccol[:], ACT.Silu).then_inc(csilu_ready, 1)
                    norm.std_scalar(act, 0)
                    copy_parts(0)
                    copy_parts(1)
                    weights(0)
                    act.wait_ge(mod_read, 2)
                    norm.h_scalar(act, 0)
                    weights(1)
                    weights(2)
                    for b in range(NB):
                        block_order(b, item, modulate, {2: lambda nb: norm.std_scalar(act, nb),
                                                        HALF - 1: lambda nb: norm.h_scalar(act, nb)})

                @block.vector
                def _(dve):
                    def modulate(q):
                        i, second = 2 + q // 2, q % 2
                        if second:
                            take_sum(i)

                    def take_sum(i):
                        l, vec = VECTORS[i]
                        dve.wait_ge(mod_sum, i + 1)
                        if vec not in (GA, GB):
                            nc.vector.tensor_scalar(mod_cols[:, l, vec, :], bank[7][:, 0:KT],
                                                    1.0 if vec in (CA, CB) else 0.0, None,
                                                    ALU.add).then_inc(mod_read, 1)
                            return
                        done = 4 * (2 * l + (vec == GB))
                        if done:
                            dve.wait_ge(gate_step, done)
                        nc.vector.tensor_scalar(gate_sign[:], bank[7][:], 0.0, 2.0, ALU.is_ge, ALU.mult).then_inc(gate_step, 1)
                        nc.vector.tensor_scalar(gate_size[:], bank[7][:], -1.0, 0.25, ALU.mult, ALU.max).then_inc(gate_step, 1)
                        dve.wait_ge(gate_step, done + 2)
                        nc.vector.tensor_tensor(gate_size[:], bank[7][:], gate_size[:], ALU.max).then_inc(gate_step, 1)
                        dve.wait_ge(gate_step, done + 3)
                        nc.vector.scalar_tensor_tensor(out=gate_rows[:, l, int(vec == GB), :], in0=gate_sign[:],
                                                       scalar=-1.0, in1=gate_size[:], op0=ALU.add,
                                                       op1=ALU.mult).then_inc(gate_step, 1)
                        dve.wait_ge(gate_step, done + 4)
                        dve.sem_inc(mod_read, 1)

                    def item(b, m):
                        n = PER * b + m
                        src = bank[2 + n % 4][:]
                        if m < 2 * G:
                            e = 2 * G * b + m
                            if e == 0:
                                dve.wait_ge(bias_loaded, 32)
                            dve.wait_ge(qk_hi_ready, e + 1)
                            if e >= 2:
                                dve.wait_ge(qk_stored[e % 2], 32 * (e // 2))
                            nc.vector.scalar_tensor_tensor(out=out_lo[:, e % 2, :], in0=src,
                                                           scalar=bias_cols[:, m:m + 1], in1=out_hi[:, e % 2, :],
                                                           op0=ALU.add, op1=ALU.subtract).then_inc(qkv_out, 1)
                            dve.wait_ge(qkv_out, n + 1)
                            dve.sem_inc(qk_lo_ready, 1)
                        else:
                            dve.wait_ge(qkv_done, n + 1)
                            if b == 2 and m == 2 * G:
                                dve.wait_ge(mod_mm, len(VECTORS))
                            nc.vector.tensor_tensor(v[:, TB * b + m - 2 * G, :], src, bias_v[:],
                                                    ALU.add).then_inc(qkv_out, 1)

                    def stats(b):
                        dve.wait_ge(x_loaded[b], 16)
                        norm.stats_vector(dve, b)

                    def weights(i):
                        if i == 0:
                            for k in range(KT):
                                dve.wait_ge(w_hi_ready, k + 1)
                                nc.vector.tensor_tensor(w_lo[:, 0, k, :], w_raw[0][:, k, :], w_hi[:, 0, k, :],
                                                        ALU.subtract).then_inc(w_ready, 1)
                            return
                        dve.wait_ge(w_hi_ready, KT + i)
                        nc.vector.tensor_tensor(w_lo[:, i, :, :], w_raw[i], w_hi[:, i, :, :],
                                                ALU.subtract).then_inc(w_ready, 1)
                    dve.wait_ge(csilu_ready, 1)
                    nc.vector.tensor_copy(cwide[:], csilu[:].unsqueeze(3).broadcast_to([P, 2, KT, 32])).then_inc(cwide_ready, 1)
                    dve.wait_ge(x_loaded[0], 16)
                    norm.stats_vector(dve, 0)
                    norm.z_vector(dve, 0)
                    dve.wait_ge(const_loaded, 16)
                    nc.vector.tensor_copy(ident[:], stage[:, 0:P])
                    nc.vector.tensor_copy(ident16[:], stage[:, 0:P])
                    nc.vector.tensor_copy(hadamard[:], stage[:, P:2 * P])
                    nc.vector.tensor_copy(mask_keys[:], stage[:, 2 * P:4 * P])
                    nc.vector.tensor_copy(mask_queries[:], stage[:, 4 * P:6 * P]).then_inc(const_ready, 1)
                    take_sum(0)
                    take_sum(1)
                    weights(0)
                    norm.split_vector(dve, 0)
                    weights(1)
                    weights(2)
                    for b in range(NB):
                        block_order(b, item, modulate, {1: stats, 3: lambda nb: norm.z_vector(dve, nb),
                                                        HALF - 1: lambda nb: norm.split_vector(dve, nb)})

        ctx0 = tokens_b[:, :].rearrange("p (g t) -> p g t", g=G)
        with ExitStack() as ctx:
            v = tokens_a
            QS = 4
            kst = sb(ctx, "kst", [P, 2, 4, S], F32R)
            qst = sb(ctx, "qst", [P, QS, 4, 512], F32R)
            probs = sb(ctx, "probs", [P, 3, 2, 512])
            ones = sb(ctx, "ones", [P, HD])
            part_max = sb(ctx, "part_max", [P, 2, 4 * TB, NB])
            neg_max = sb(ctx, "neg_max", [P, 4 * TB])
            neg_hi = sb(ctx, "neg_hi", [P, 4 * TB], F32R)
            neg_parts = sb(ctx, "neg_parts", [P, 2 * 4 * TB])
            max_rows = sb(ctx, "max_rows", [2 * 4 * TB, 2, P], F32R)
            o_copy = sb(ctx, "o_copy", [P, 512])
            sum_copy = sb(ctx, "sum_copy", [P, 512])
            FW = 64
            fw = [sb(ctx, f"fw{i}", [P, H0 // P, FW]) for i in range(2)]
            NQ = G * NB
            k_loaded = [[sem(ctx, f"k_loaded{i}_{j}") for j in range(NB)] for i in range(2)]
            q_loaded = [sem(ctx, f"q_loaded{i}") for i in range(QS)]
            max_stored = [sem(ctx, f"max_stored{i}") for i in range(QS)]
            ones_ready = sem(ctx, "ones_ready")
            max_mm = sem(ctx, "max_mm")
            max_read = sem(ctx, "max_read")
            max_chain = sem(ctx, "max_chain")
            rows_ready = sem(ctx, "max_rows_ready")
            rows_stored = sem(ctx, "max_rows_stored")
            score_mm = sem(ctx, "score_mm")
            exp_done = sem(ctx, "exp_done")
            pv_done = sem(ctx, "pv_done")
            copied = sem(ctx, "copied")
            o_copied = sem(ctx, "o_copied")
            rec_done = sem(ctx, "rec_done")
            ctx_done = sem(ctx, "ctx_done")
            fw_loaded = sem(ctx, "fw_loaded")
            fw_step = sem(ctx, "fw_step")
            fw_stored = sem(ctx, "fw_stored")

            def slots_before(n):
                g, j = divmod(n, NB)
                return g * (4 * TB * NB * (NB + 1) // 2 + NB) + 4 * TB * j * (j + 1) // 2 + j

            def pairs_before(n):
                g, j = divmod(n, NB)
                return g * (2 * TB * NB * (NB + 1) // 2) + 2 * TB * j * (j + 1) // 2

            LEAD = 6
            PRELUDE = slots_before(1) + 10

            def schedule():
                done, rested = PRELUDE, set()
                goals = [(pairs_before(n) - LEAD, slots_before(n + 1)) for n in range(1, NQ)]
                turns = [goal - 1 for _, goal in goals]
                for n in range(NQ):
                    for i in range(pairs_before(n + 1) - pairs_before(n)):
                        at = pairs_before(n) + i
                        need = [-(-(goal - done) // max(by - at, 1)) for by, goal in goals if goal > done]
                        now = max([0] + need)
                        for turn in turns:
                            if done < turn < done + now:
                                now = turn - done
                            elif done == turn:
                                now = 1 if turn in rested else 0
                                rested.add(turn)
                        yield n, i, range(done, done + now)
                        done += now

            def slot_of(slot):
                n = max(m for m in range(NQ) if slots_before(m) <= slot)
                return n, slot - slots_before(n)

            with nc.Block() as block:
                @block.sync
                def _(sp):
                    for n in range(NQ):
                        g, j = divmod(n, NB)
                        cols = slice(512 * j, 512 * j + 512)
                        if n == QS:
                            load_early_projection(sp, a["w_out0"], 0)
                        if n >= QS:
                            sp.wait_ge(score_mm, 2 * pairs_before(n - QS + 1))
                        if g >= 2 and j == 0:
                            sp.wait_ge(score_mm, 2 * pairs_before(NB * (g - 1)))
                        for part, (qs, ks) in enumerate(((q_hi, k_hi), (q_hi, k_lo), (q_lo, k_hi))):
                            rows = slice(HD * part, HD * part + HD)
                            sp.dma_start(qst[rows, n % QS, :, :].bitcast(F32),
                                         qs[g, :, cols].rearrange("(h d) t -> d h t", h=4)).then_inc(q_loaded[n % QS], 16)
                            sp.dma_start(kst[rows, g % 2, :, cols].bitcast(F32),
                                         ks[g, :, cols].rearrange("(h d) t -> d h t", h=4)).then_inc(k_loaded[g % 2][j], 16)

                @block.gpsimd
                def _(pool):
                    w2 = a["w2t"].rearrange("(c p) d -> p c d", p=P)
                    w2m = w2_mixed.rearrange("(c p) d -> p c d", p=P)

                    def butterflies(s):
                        cols = slice(FW * s, FW * s + FW)
                        if s:
                            pool.wait_ge(fw_stored, 16 * s)
                        pool.dma_start(fw[0][:], w2[:, :, cols]).then_inc(fw_loaded, 16)
                        pool.wait_ge(fw_loaded, 16 * (s + 1))
                        for r in range(4):
                            half = 1 << r
                            src = fw[r % 2][:].rearrange("p (a b h) d -> p a b (h d)", b=2, h=half)
                            dst = fw[1 - r % 2][:].rearrange("p (a b h) d -> p a b (h d)", b=2, h=half)
                            nc.gpsimd.tensor_tensor(dst[:, :, 0, :], src[:, :, 0, :], src[:, :, 1, :], ALU.add).then_inc(fw_step, 1)
                            nc.gpsimd.tensor_tensor(dst[:, :, 1, :], src[:, :, 0, :], src[:, :, 1, :], ALU.subtract).then_inc(fw_step, 1)
                            pool.wait_ge(fw_step, 8 * s + 2 * r + 2)
                        pool.dma_start(w2m[:, :, cols], fw[0][:]).then_inc(fw_stored, 16)
                    nc.gpsimd.memset(ones[:], 1.0).then_inc(ones_ready, 1)
                    for g in range(2):
                        for j in range(NB):
                            pool.wait_ge(ones_ready, NB * g + j + 1)
                            nc.gpsimd.memset(kst[BIASROW:BIASROW + 2, g, :, 512 * j:512 * j + 512].bitcast(F32),
                                             1.0).then_inc(ones_ready, 1)
                    for n in range(NQ):
                        pool.wait_ge(rows_ready, n + 1)
                        if n >= QS:
                            pool.wait_ge(score_mm, 2 * pairs_before(n - QS + 1))
                        pool.dma_start(max_dram[n % 2], max_rows[:, n % 2, :].bitcast(F32)).then_inc(rows_stored, 16)
                        pool.wait_ge(rows_stored, 16 * (n + 1))
                        pool.dma_start(qst[BIASROW:BIASROW + 2, n % QS, :, :].bitcast(F32),
                                       max_dram[n % 2].rearrange("(part h t) q -> part h (t q)", part=2, h=4)
                                       ).then_inc(max_stored[n % QS], 16)
                        if 2 <= n < 2 + D // FW:
                            butterflies(n - 2)
                    pool.wait_ge(fw_stored, 16 * (D // FW))

                @block.tensor
                def _(pe):
                    def max_step(n, i):
                        g, j = divmod(n, NB)
                        slot = slots_before(n) + i
                        dst = bank[slot % 3]
                        if i == 0:
                            pe.wait_ge(q_loaded[n % QS], 48 * (n // QS + 1))
                            pe.wait_ge(k_loaded[g % 2][j], 48 * (g // 2 + 1))
                        if slot >= 3:
                            pe.wait_ge(max_read, slot - 2)
                        if i == 4 * TB * (j + 1):
                            pe.wait_ge(max_chain, 4 * n + 4)
                            nc.tensor.transpose(dst[0:2 * 4 * TB, 0:P], neg_parts[:], ident[:]).then_inc(max_mm, 1)
                            return
                        ht, c = divmod(i, j + 1)
                        h, t = divmod(ht, TB)
                        wide = 512 if c < j else max(P * (t + 1), 2 * P)
                        mm = nc.tensor.matmul(dst[:, 0:wide], qst[0:BIASROW, n % QS, h, P * t:P * t + P],
                                              kst[0:BIASROW, g % 2, h, 512 * c:512 * c + wide],
                                              start=True, stop=(c < j))
                        if c == j:
                            at = P * t
                            mw = 2 * P if t == 0 else P
                            mm = nc.tensor.matmul(dst[:, at:at + mw], ident16[:], mask_queries[:, 0:mw],
                                                  start=False, stop=True)
                        mm.then_inc(max_mm, 1)

                    def score(n, i):
                        g, j = divmod(n, NB)
                        kt, pair = divmod(i, 2)
                        sp_ = pairs_before(n) + i
                        if i == 0:
                            pe.wait_ge(max_stored[n % QS], 16 * (n // QS + 1))
                            pe.wait_ge(ones_ready, 2 * NB + 1)
                        t = kt - TB * j
                        c0 = min(P * max(t, 0), 2 * P)
                        for u in range(2):
                            h = 2 * pair + u
                            sh = 2 * sp_ + u
                            dst = bank[3 + sh % 3]
                            if sh >= 3:
                                pe.wait_ge(exp_done, sh - 2)
                            mm = nc.tensor.matmul(dst[:, c0:512], kst[0:BIASROW + 2, g % 2, h, P * kt:P * kt + P],
                                                  qst[0:BIASROW + 2, n % QS, h, c0:512], start=True, stop=(t < 0))
                            if t >= 0:
                                mw = 2 * P if t == 3 else P
                                mm = nc.tensor.matmul(dst[:, c0:c0 + mw], ident16[:], mask_keys[:, 2 * P - mw:2 * P],
                                                      start=False, stop=True)
                            mm.then_inc(score_mm, 1)

                    def context(n, i):
                        g, j = divmod(n, NB)
                        kt, pair = divmod(i, 2)
                        sp_ = pairs_before(n) + i
                        if i == 0 and n:
                            pe.wait_ge(copied, 2 * n)
                            pe.wait_ge(o_copied, n)
                        pe.wait_ge(exp_done, 2 * sp_ + 2)
                        c0 = P * max(kt - TB * j, 0)
                        first, last = kt == 0, kt == TB * (j + 1) - 1
                        for u in range(2):
                            h = 2 * pair + u
                            nc.tensor.matmul(bank[6][HD * h:HD * h + HD, c0:512],
                                             v[:, kt, HD * (4 * g + h):HD * (4 * g + h) + HD],
                                             probs[:, sp_ % 3, u, c0:512], start=first, stop=last)
                        for u in range(2):
                            h = (2 * pair + u + 2) % 4
                            mm = nc.tensor.matmul(bank[7][HD * h:HD * h + HD, c0:512], ones[:],
                                                  probs[:, sp_ % 3, u, c0:512], start=first, stop=last)
                        mm.then_inc(pv_done, 1)

                    for slot in range(PRELUDE):
                        max_step(*slot_of(slot))
                    late = None
                    for n, i, slots in schedule():
                        first = len(slots) // 2
                        score(n, i)
                        for slot in slots[:first]:
                            max_step(*slot_of(slot))
                        if late:
                            context(*late)
                        for slot in slots[first:]:
                            max_step(*slot_of(slot))
                        late = (n, i)
                    context(*late)

                @block.scalar
                def _(act):
                    def copies(n):
                        act.wait_ge(pv_done, pairs_before(n + 1))
                        if n:
                            act.wait_ge(ctx_done, 4 * n)
                        nc.scalar.copy(sum_copy[0:64, :], bank[7][64:128, :]).then_inc(copied, 1)
                        nc.scalar.copy(sum_copy[64:128, :], bank[7][0:64, :]).then_inc(copied, 1)
                    for n in range(NQ):
                        j = n % NB
                        for i in range(pairs_before(n + 1) - pairs_before(n)):
                            sp_ = pairs_before(n) + i
                            c0 = P * max(i // 2 - TB * j, 0)
                            if sp_ >= 3:
                                act.wait_ge(pv_done, sp_ - 2)
                            for u in range(2):
                                sh = 2 * sp_ + u
                                act.wait_ge(score_mm, sh + 1)
                                nc.scalar.activation(probs[:, sp_ % 3, u, c0:512], bank[3 + sh % 3][:, c0:512],
                                                     ACT.Exp, scale=SCALE).then_inc(exp_done, 1)
                            if i == 0 and n:
                                copies(n - 1)
                    copies(NQ - 1)

                @block.vector
                def _(dve):

                    def max_step(n, i):
                        g, j = divmod(n, NB)
                        slot = slots_before(n) + i
                        if i == 4 * TB * (j + 1):
                            parts = 4 * TB
                            dve.wait_ge(max_read, slot)
                            nc.vector.tensor_reduce(neg_max[:], part_max[:, n % 2, :, 0:j + 1], AX_X, ALU.max,
                                                    negate=True).then_inc(max_chain, 1)
                            dve.wait_ge(max_chain, 4 * n + 1)
                            nc.vector.tensor_copy(neg_hi[:], neg_max[:]).then_inc(max_chain, 1)
                            dve.wait_ge(max_chain, 4 * n + 2)
                            nc.vector.tensor_copy(neg_parts[:, 0:parts], neg_hi[:]).then_inc(max_chain, 1)
                            nc.vector.tensor_tensor(neg_parts[:, parts:2 * parts], neg_max[:], neg_hi[:],
                                                    ALU.subtract).then_inc(max_chain, 1)
                            dve.wait_ge(max_mm, slot + 1)
                            if n >= 2:
                                dve.wait_ge(max_stored[(n - 2) % QS], 16 * ((n - 2) // QS + 1))
                            nc.vector.tensor_copy(max_rows[:, n % 2, :], bank[slot % 3][0:2 * parts, 0:P]).then_inc(max_read, 1)
                            dve.wait_ge(max_read, slot + 1)
                            dve.sem_inc(rows_ready, 1)
                            return
                        ht, c = divmod(i, j + 1)
                        t = ht % TB
                        wide = 512 if c < j else max(P * (t + 1), 2 * P)
                        dve.wait_ge(max_mm, slot + 1)
                        nc.vector.tensor_reduce(part_max[:, n % 2, ht, c:c + 1], bank[slot % 3][:, 0:wide], AX_X,
                                                ALU.max).then_inc(max_read, 1)

                    def normalise(n, part):
                        g, j = divmod(n, NB)
                        c = slice(P * part, P * part + P)
                        if part == 0:
                            dve.wait_ge(copied, 2 * n + 2)
                        nc.vector.reciprocal(sum_copy[:, c], sum_copy[:, c]).then_inc(rec_done, 1)
                        dve.wait_ge(rec_done, 4 * n + part + 1)
                        nc.vector.tensor_tensor(ctx0[:, g, 512 * j + P * part:512 * j + P * part + P],
                                                o_copy[:, c], sum_copy[:, c],
                                                ALU.mult).then_inc(ctx_done, 1)

                    def copy_out(n):
                        dve.wait_ge(pv_done, pairs_before(n + 1))
                        if n:
                            dve.wait_ge(ctx_done, 4 * n)
                        nc.vector.tensor_copy(o_copy[:], bank[6][:]).then_inc(o_copied, 1)

                    for slot in range(PRELUDE):
                        max_step(*slot_of(slot))
                    for n, i, slots in schedule():
                        first = len(slots) // 2
                        for slot in slots[:first]:
                            max_step(*slot_of(slot))
                        if n and i == 0:
                            copy_out(n - 1)
                        for slot in slots[first:]:
                            max_step(*slot_of(slot))
                        if n and 2 <= i < 6:
                            normalise(n - 1, i - 2)
                    copy_out(NQ - 1)
                    for part in range(4):
                        normalise(NQ - 1, part)

        def project_out(ctx, tag, there, next_w, bias, src, src_ready, res_ready):
            raw, gate = early_square, early_gate[:]
            bias_row = sb(ctx, tag + "bias", [P, D])
            w_hi = sb(ctx, tag + "w_hi", [P, KT, D], F32R)
            w_lo = sb(ctx, tag + "w_lo", [P, KT, D], F32R)
            c_hi = sb(ctx, tag + "c_hi", [P, 2, G, 2 * P], F32R)
            c_lo = sb(ctx, tag + "c_lo", [P, 2, G, 2 * P], F32R)
            bias_loaded = sem(ctx, tag + "bias_loaded")
            gated = sem(ctx, tag + "w_gated_s")
            bias_gated = sem(ctx, tag + "bias_gated")
            w_hi_s = sem(ctx, tag + "w_hi_s")
            w_ready = sem(ctx, tag + "w_ready")
            hi_s = sem(ctx, tag + "c_hi_s")
            c_ready = sem(ctx, tag + "c_ready")
            xb_ready = sem(ctx, tag + "xb_ready")
            proj = sem(ctx, tag + "proj")
            x_ready = sem(ctx, tag + "x_ready")

            class Parts:
                ready = x_ready

                def sync(sp):
                    sp.dma_start(bias_row[:], bias.broadcast_to([P, D])).then_inc(bias_loaded, 16)

                def next_sync(sp):
                    sp.wait_ge(w_ready, KT)
                    load_early_pair(sp, *next_w)
                    sp.wait_ge(early_loaded, there + 32)

                def weights_scalar(act):
                    for k in range(KT):
                        act.wait_ge(gated, k + 1)
                        nc.scalar.copy(w_hi[:, k, :], raw[:, k, :]).then_inc(w_hi_s, 1)

                def weights_vector(dve):
                    def lo(k):
                        dve.wait_ge(w_hi_s, k + 1)
                        nc.vector.tensor_tensor(w_lo[:, k, :], raw[:, k, :], w_hi[:, k, :], ALU.subtract).then_inc(w_ready, 1)
                    dve.wait_ge(early_loaded, there)
                    for k in range(KT):
                        nc.vector.tensor_tensor(raw[:, k, :], raw[:, k, :], gate, ALU.mult).then_inc(gated, 1)
                        if k:
                            lo(k - 1)
                    lo(KT - 1)
                    dve.wait_ge(bias_loaded, 16)
                    nc.vector.tensor_tensor(bias_row[:], bias_row[:], gate, ALU.mult).then_inc(bias_gated, 1)

                def bias_gpsimd(pool):
                    pool.wait_ge(bias_gated, 1)
                    for t in range(T):
                        res_ready(pool, t)
                        nc.gpsimd.tensor_tensor(x[:, t, :], x[:, t, :], bias_row[:], ALU.add).then_inc(xb_ready, 1)

                def half(i):
                    return src[:, :, 2 * P * i:2 * P * i + 2 * P]

                def hi_scalar(act, i):
                    src_ready(act, i // 2)
                    if i >= 2:
                        act.wait_ge(proj, 2 * (i - 1))
                    nc.scalar.copy(c_hi[:, i % 2, :, :], Parts.half(i)).then_inc(hi_s, 1)

                def lo_vector(dve, i):
                    dve.wait_ge(hi_s, i + 1)
                    nc.vector.tensor_tensor(c_lo[:, i % 2, :, :], Parts.half(i), c_hi[:, i % 2, :, :],
                                            ALU.subtract).then_inc(c_ready, 1)

                def tensor(pe, i):
                    pe.wait_ge(c_ready, i + 1)
                    for t in range(2):
                        n = 2 * i + t
                        if n >= 4:
                            pe.wait_ge(x_ready, n - 3)
                        c = slice(P * t, P * t + P)
                        for g in range(G):
                            if n == 0:
                                pe.wait_ge(w_ready, g + 1)
                            mm = product(bank[2 + n % 4][:], lambda _: (c_hi[:, i % 2, g, c], c_lo[:, i % 2, g, c]),
                                         lambda _: (w_hi[:, g, :], w_lo[:, g, :]), 1, first=(g == 0), last=(g == G - 1))
                        mm.then_inc(proj, 1)

                def add_vector(dve, i):
                    for n in (2 * i, 2 * i + 1):
                        dve.wait_ge(proj, n + 1)
                        dve.wait_ge(xb_ready, n + 1)
                        nc.vector.tensor_tensor(x[:, n, :], bank[2 + n % 4][:], x[:, n, :], ALU.add).then_inc(x_ready, 1)
            return Parts

        def nothing(engine, b, part):
            pass

        def projection_and_norm(out_p, norm, more_tensor=nothing, more_vector=nothing):

            def tensor(pe):
                for b in range(NB):
                    for part in range(2):
                        if b + 1 < NB:
                            more_tensor(pe, b + 1, part)
                        out_p.tensor(pe, 2 * b + part)
                    if b:
                        norm.tensor(pe, b - 1)
                norm.tensor(pe, NB - 1)

            def scalar(act):
                for b in range(NB):
                    out_p.hi_scalar(act, 2 * b + 1)
                    if b:
                        norm.std_scalar(act, b - 1)
                    if b + 1 < NB:
                        out_p.hi_scalar(act, 2 * b + 2)
                    if b:
                        norm.h_scalar(act, b - 1)
                norm.std_scalar(act, NB - 1)
                norm.h_scalar(act, NB - 1)

            def statistics(dve, b):
                dve.wait_ge(out_p.ready, TB * (b + 1))
                norm.stats_vector(dve, b)
                norm.z_vector(dve, b)

            def vector(dve):
                for b in range(NB):
                    out_p.lo_vector(dve, 2 * b + 1)
                    if b:
                        out_p.add_vector(dve, 2 * b - 1)
                    if b + 1 < NB:
                        more_vector(dve, b + 1, 0)
                    if b:
                        statistics(dve, b - 1)
                    if b + 1 < NB:
                        more_vector(dve, b + 1, 1)
                    out_p.add_vector(dve, 2 * b)
                    if b + 1 < NB:
                        out_p.lo_vector(dve, 2 * b + 2)
                        if b:
                            norm.split_vector(dve, b - 1)
                dve.wait_ge(out_p.ready, TB * NB - 2)
                norm.half_stats_vector(dve, NB - 1, 0)
                out_p.add_vector(dve, 2 * NB - 1)
                dve.wait_ge(out_p.ready, TB * NB)
                norm.stats_vector(dve, NB - 1, halves=(1,))
                norm.split_vector(dve, NB - 2)
                norm.z_vector(dve, NB - 1)
                norm.split_vector(dve, NB - 1)
            return tensor, scalar, vector

        def feed_forward(tag, layer, there, gate_w, up_w, down_w, hidden, ht, gate_s=None, up_s=None,
                         down_s=None, store=None, next_w=None):
            nch = hidden // P
            segs = [list(range(c, min(c + 2, nch))) for c in range(0, nch, 2)]
            mixed = down_s is None
            steps = [(s, b) for s in range(len(segs)) for b in range(NB)]
            ubase = [0]
            for s, b in steps:
                ubase.append(ubase[-1] + len(segs[s]))
            with ExitStack() as ctx:
                def part(at, outer, inner):
                    return tokens_b[:, at:at + outer * inner].rearrange("p (o i) -> p o i", o=outer)
                raw_g, raw_u = part(0, KT, 2 * P), part(1024, KT, 2 * P)
                raws = lambda s: (raw_g, raw_u) if s else (early_pair[:, 0, :, :], early_pair[:, 1, :, :])
                raw_d, down = part(2048, 2, D), part(3072, 2, D)
                silu, act_ = part(4096, 2, 512), part(5120, 2, 512)
                drow = tokens_b[:, 6144:6144 + D]
                gate = tokens_b[:, 6656:6656 + D]
                wh = [sb(ctx, tag + f"w{n}_hi", [P, 2, KT, 2 * P], F32R) for n in "gu"]
                wl = [sb(ctx, tag + f"w{n}_lo", [P, 2, KT, 2 * P], F32R) for n in "gu"]
                dh = sb(ctx, tag + "d_hi", [P, 2, 2, D], F32R)
                dl = sb(ctx, tag + "d_lo", [P, 2, 2, D], F32R)
                if not mixed:
                    gs = sb(ctx, tag + "gs", [P, nch])
                    us = sb(ctx, tag + "us", [P, nch])
                hh = sb(ctx, tag + "hid_hi", [P, 2, 2, 512], F32R)
                hl = sb(ctx, tag + "hid_lo", [P, 2, 2, 512], F32R)
                gate_loaded = sem(ctx, tag + "gate_loaded")
                scales_loaded = sem(ctx, tag + "scales_loaded")
                drow_ready = sem(ctx, tag + "drow_ready")
                gu_loaded = sem(ctx, tag + "gu_loaded")
                d_loaded = sem(ctx, tag + "d_loaded")
                gu_hi = sem(ctx, tag + "gu_hi")
                gu_ready = sem(ctx, tag + "gu_ready")
                b_hi_s = sem(ctx, tag + "b_hi_s")
                b_ready = sem(ctx, tag + "b_ready")
                mix_mm = sem(ctx, tag + "mix_mm")
                down_s_ = sem(ctx, tag + "down_scaled")
                d_hi_s = sem(ctx, tag + "d_hi_s")
                d_ready = sem(ctx, tag + "d_ready")
                up_mm = sem(ctx, tag + "up_mm")
                silu_s = sem(ctx, tag + "silu_s")
                hid_s = sem(ctx, tag + "hid_s")
                hh_s = sem(ctx, tag + "hh_s")
                hl_s = sem(ctx, tag + "hl_s")
                down_mm = sem(ctx, tag + "down_mm")
                x_added = sem(ctx, tag + "x_added")
                chunks_before = [2 * s for s in range(len(segs))]

                def gu_pieces(s):
                    parts = [slice(k, k + 1) for k in range(KT)] if s == 0 else [slice(0, KT)]
                    return [(m, chunks) for m in range(2) for chunks in parts]

                def gu_before(s):
                    return sum(len(gu_pieces(q)) for q in range(s))

                with nc.Block() as block:
                    @block.sync
                    def _(sp):
                        sp.dma_start(gate, gates[2 * layer + 1:2 * layer + 2, :].broadcast_to([P, D])).then_inc(gate_loaded, 16)
                        for s, seg in enumerate(segs):
                            w = len(seg) * P
                            c = slice(seg[0] * P, seg[0] * P + w)
                            if s >= 2:
                                sp.wait_ge(gu_ready, gu_before(s))
                            if s:
                                sp.dma_start(raw_g[:, :, 0:w], tile_rows(gate_w)[:, :, c]).then_inc(gu_loaded, 16)
                                sp.dma_start(raw_u[:, :, 0:w], tile_rows(up_w)[:, :, c]).then_inc(gu_loaded, 16)
                            if s == 1 and next_w is not None:
                                sp.wait_ge(gu_ready, gu_before(1))
                                sp.dma_start(early_square, tile_rows(next_w)).then_inc(early_loaded, 16)
                            if s == 0 and not mixed:
                                sp.dma_start(gs[:], gate_s).then_inc(scales_loaded, 16)
                                sp.dma_start(us[:], up_s).then_inc(scales_loaded, 16)
                                sp.dma_start(drow, down_s.broadcast_to([P, D])).then_inc(scales_loaded, 16)
                            if s:
                                if mixed:
                                    sp.wait_ge(b_ready, s)
                                else:
                                    sp.wait_ge(down_s_, chunks_before[s])
                            sp.dma_start(raw_d[:, 0:len(seg), :], tile_rows(down_w[c, :])).then_inc(d_loaded, 16)
                        if store is not None:
                            last = len(steps) - NB
                            for b in range(NB):
                                for t in range(TB):
                                    sp.wait_ge(x_added, TB * (last + b) + t + 1)
                                    sp.dma_start(store[(TB * b + t) * P:(TB * b + t + 1) * P, :],
                                                 x[:, TB * b + t, :]).then_inc(stored, 16)
                            sp.wait_ge(stored, 16 * T)

                    @block.tensor
                    def _(pe):
                        def mix(s, c):
                            n = chunks_before[s] + c
                            pe.wait_ge(b_ready, s + 1)
                            if n:
                                pe.wait_ge(down_s_, n)
                            nc.tensor.matmul(bank[7][:], hadamard[:], dh[:, s % 2, c, :], start=True, stop=False)
                            nc.tensor.matmul(bank[7][:], hadamard[:], dl[:, s % 2, c, :], start=False,
                                             stop=True).then_inc(mix_mm, 1)

                        def up(k):
                            s, b = steps[k]
                            cols = slice(512 * b, 512 * b + 512)
                            for c in range(len(segs[s])):
                                u = ubase[k] + c
                                if u >= 2:
                                    pe.wait_ge(hid_s, u - 1)
                                wc = slice(P * c, P * c + P)
                                for m in range(2):
                                    if s and b == 0 and c == 0:
                                        pe.wait_ge(gu_ready, gu_before(s) + m + 1)
                                    mm = product(bank[2 * (u % 2) + m][:],
                                                 lambda i: (wh[m][:, s % 2, i, wc], wl[m][:, s % 2, i, wc]),
                                                 lambda i: (ht[0][:, i, cols], ht[1][:, i, cols]), KT,
                                                 before=(lambda i: pe.wait_ge(gu_ready, KT * m + i + 1)) if k == c == 0 else None)
                                mm.then_inc(up_mm, 1)

                        def down_(k):
                            s, b = steps[k]
                            pe.wait_ge(d_ready, chunks_before[s] + len(segs[s]))
                            pe.wait_ge(hl_s, ubase[k + 1])
                            for t in range(TB):
                                n = TB * k + t
                                if n >= 3:
                                    pe.wait_ge(x_added, n - 2)
                                tc = slice(P * t, P * t + P)
                                product(bank[4 + n % 3][:],
                                        lambda i: (hh[:, k % 2, i, tc], hl[:, k % 2, i, tc]),
                                        lambda i: (dh[:, s % 2, i, :], dl[:, s % 2, i, :]),
                                        len(segs[s])).then_inc(down_mm, 1)

                        for k, (s, b) in enumerate(steps):
                            up(k)
                            if mixed and k == 0:
                                mix(0, 0)
                                mix(0, 1)
                            ahead = mixed and b == 2 and s + 1 < len(segs)
                            if ahead:
                                mix(s + 1, 0)
                            if k:
                                down_(k - 1)
                            if ahead:
                                mix(s + 1, 1)
                        down_(len(steps) - 1)

                    @block.scalar
                    def _(act):
                        def weights(s):
                            w = len(segs[s]) * P
                            if s:
                                act.wait_ge(gu_loaded, 32 * s)
                            else:
                                act.wait_ge(early_loaded, there)
                            if s >= 2:
                                act.wait_ge(up_mm, ubase[NB * (s - 1)])
                            for m, ks in gu_pieces(s):
                                nc.scalar.copy(wh[m][:, s % 2, ks, 0:w], raws(s)[m][:, ks, 0:w]).then_inc(gu_hi, 1)
                            if mixed:
                                act.wait_ge(d_loaded, 16 * (s + 1))
                                if s >= 2:
                                    act.wait_ge(down_mm, TB * NB * (s - 1))
                                nc.scalar.copy(dh[:, s % 2, :, :], raw_d).then_inc(b_hi_s, 1)

                        def hidden_hi(k, c):
                            u = ubase[k] + c
                            act.wait_ge(hid_s, u + 1)
                            if k >= 2:
                                act.wait_ge(down_mm, TB * (k - 1))
                            nc.scalar.copy(hh[:, k % 2, c, :], act_[:, u % 2, :]).then_inc(hh_s, 1)

                        weights(0)
                        if not mixed:
                            act.wait_ge(scales_loaded, 48)
                        late = None
                        for k, (s, b) in enumerate(steps):
                            if b == 1 and s + 1 < len(segs):
                                weights(s + 1)
                            for c, ch in enumerate(segs[s]):
                                u = ubase[k] + c
                                act.wait_ge(up_mm, u + 1)
                                if u >= 2:
                                    act.wait_ge(hid_s, u - 1)
                                nc.scalar.activation(silu[:, u % 2, :], bank[2 * (u % 2)][:], ACT.Silu,
                                                     scale=1.0 if mixed else gs[:, ch:ch + 1]).then_inc(silu_s, 1)
                                if late:
                                    hidden_hi(*late)
                                late = (k, c)
                            if len(segs[s]) == 1:
                                hidden_hi(*late)
                                late = None
                        if late:
                            hidden_hi(*late)

                    @block.vector
                    def _(dve):

                        def weights(s):
                            w = len(segs[s]) * P
                            for piece, (m, ks) in enumerate(gu_pieces(s)):
                                dve.wait_ge(gu_hi, gu_before(s) + piece + 1)
                                nc.vector.tensor_tensor(wl[m][:, s % 2, ks, 0:w], raws(s)[m][:, ks, 0:w],
                                                        wh[m][:, s % 2, ks, 0:w], ALU.subtract).then_inc(gu_ready, 1)
                            if mixed:
                                dve.wait_ge(b_hi_s, s + 1)
                                nc.vector.tensor_tensor(dl[:, s % 2, :, :], raw_d, dh[:, s % 2, :, :], ALU.subtract).then_inc(b_ready, 1)
                            else:
                                dve.wait_ge(d_loaded, 16 * (s + 1))

                        def down_weights(s, c):
                            n = chunks_before[s] + c
                            if s >= 2:
                                dve.wait_ge(down_mm, TB * NB * (s - 1))
                            if mixed:
                                dve.wait_ge(mix_mm, n + 1)
                            src = bank[7][:] if mixed else raw_d[:, c, :]
                            nc.vector.tensor_tensor(down[:, c, :], src, drow, ALU.mult).then_inc(down_s_, 1)
                            dve.wait_ge(down_s_, n + 1)
                            nc.vector.tensor_copy(dh[:, s % 2, c, :], down[:, c, :]).then_inc(d_hi_s, 1)
                            dve.wait_ge(d_hi_s, n + 1)
                            nc.vector.tensor_tensor(dl[:, s % 2, c, :], down[:, c, :], dh[:, s % 2, c, :],
                                                    ALU.subtract).then_inc(d_ready, 1)

                        def hidden_lo(k, c):
                            u = ubase[k] + c
                            dve.wait_ge(hh_s, u + 1)
                            nc.vector.tensor_tensor(hl[:, k % 2, c, :], act_[:, u % 2, :], hh[:, k % 2, c, :],
                                                    ALU.subtract).then_inc(hl_s, 1)

                        def add_x(k, tiles=range(TB)):
                            s, b = steps[k]
                            for t in tiles:
                                n = TB * k + t
                                dve.wait_ge(down_mm, n + 1)
                                if s:
                                    dve.wait_ge(x_added, n - TB * NB + 1)
                                xt = x[:, TB * b + t, :]
                                nc.vector.tensor_tensor(xt, bank[4 + n % 3][:], xt, ALU.add).then_inc(x_added, 1)

                        weights(0)
                        dve.wait_ge(gate_loaded, 16)
                        if mixed:
                            nc.vector.tensor_scalar(drow, gate, float(H0) ** -0.5, None, ALU.mult).then_inc(drow_ready, 1)
                        else:
                            dve.wait_ge(scales_loaded, 48)
                            nc.vector.tensor_tensor(drow, drow, gate, ALU.mult).then_inc(drow_ready, 1)
                        dve.wait_ge(drow_ready, 1)
                        late = None
                        for k, (s, b) in enumerate(steps):
                            if b == 1 and s + 1 < len(segs):
                                weights(s + 1)
                            if b == 3 and s + 1 < len(segs):
                                for c in range(1, len(segs[s + 1])):
                                    down_weights(s + 1, c)
                            for c, ch in enumerate(segs[s]):
                                u = ubase[k] + c
                                dve.wait_ge(silu_s, u + 1)
                                if u >= 2:
                                    dve.wait_ge(hh_s, u - 1)
                                    dve.wait_ge(hl_s, u - 1)
                                up_bank = bank[2 * (u % 2) + 1][:]
                                if mixed:
                                    nc.vector.tensor_tensor(act_[:, u % 2, :], up_bank, silu[:, u % 2, :],
                                                            ALU.mult).then_inc(hid_s, 1)
                                else:
                                    nc.vector.scalar_tensor_tensor(out=act_[:, u % 2, :], in0=up_bank,
                                                                   scalar=us[:, ch:ch + 1], in1=silu[:, u % 2, :],
                                                                   op0=ALU.mult, op1=ALU.mult).then_inc(hid_s, 1)
                                if late:
                                    hidden_lo(*late)
                                late = (k, c)
                            if len(segs[s]) == 1:
                                if k:
                                    add_x(k - 1, range(0, 2))
                                hidden_lo(*late)
                                late = None
                            if k == 0:
                                for c in range(len(segs[0])):
                                    down_weights(0, c)
                            if b == 2 and s + 1 < len(segs):
                                down_weights(s + 1, 0)
                            if k:
                                add_x(k - 1, range(2 if len(segs[s]) == 1 else 0, TB))
                        if late:
                            hidden_lo(*late)
                        add_x(len(steps) - 1)

        with ExitStack() as ffn:
            h2_hi = sb(ffn, "h2_hi", [P, KT, S], F32R)
            h2_lo = sb(ffn, "h2_lo", [P, KT, S], F32R)
            with ExitStack() as ctx:
                res_loaded = [sem(ctx, f"res_loaded{b}") for b in range(NB)]
                out_p = project_out(ctx, "o0_", OUT0, (a["w1t"], a["w3t"]), a["b_out0"],
                                    ctx0, lambda act, b: None,
                                    lambda pool, t: pool.wait_ge(res_loaded[t // TB], 16))
                norm = Norm(ctx, "n2_", lambda b, t: x[:, TB * b + t, :], mod_cols[:, 0, SB, :],
                            mod_cols[:, 0, CB, :], h2_hi, h2_lo, zbufs=1)
                on_tensor, on_scalar, on_vector = projection_and_norm(out_p, norm)
                with nc.Block() as block:
                    @block.sync
                    def _(sp):
                        out_p.sync(sp)
                        for b in range(NB):
                            rows = slice(TB * b, TB * b + TB)
                            sp.dma_start(x[:, rows, :], tile_rows(a["L0_attn_x"])[:, rows, :]).then_inc(res_loaded[b], 16)
                        out_p.next_sync(sp)

                    @block.gpsimd
                    def _(pool):
                        out_p.bias_gpsimd(pool)

                    @block.tensor
                    def _(pe):
                        on_tensor(pe)

                    @block.scalar
                    def _(act):
                        out_p.hi_scalar(act, 0)
                        out_p.weights_scalar(act)
                        on_scalar(act)

                    @block.vector
                    def _(dve):
                        out_p.lo_vector(dve, 0)
                        out_p.weights_vector(dve)
                        on_vector(dve)

            feed_forward("f0_", 0, FFN0, a["w1t"], a["w3t"], w2_mixed, H0, (h2_hi, h2_lo), next_w=a["w_qkv1"][0])

        with ExitStack() as ffn:
            qt = tokens_b[:, :].rearrange("p (g t) -> p g t", g=G)
            kv_cols = P + 2
            kv = sb(ffn, "kv", [P, G, P])
            k_sum = sb(ffn, "k_sum", [P, G, 32])
            with ExitStack() as ctx:
                ht_hi = sb(ctx, "ht5_hi", [P, KT, 2 * 512], F32R)
                ht_lo = sb(ctx, "ht5_lo", [P, KT, 2 * 512], F32R)
                w_hi = sb(ctx, "w5_hi", [P, 3, KT, D], F32R)
                w_lo = sb(ctx, "w5_lo", [P, 3, KT, D], F32R)
                w_raw = [early_square] + [tokens_b[:, KT * D * i:KT * D * (i + 1)].rearrange("p (k d) -> p k d", k=KT)
                                          for i in range(2)]
                bq = sb(ctx, "bq", [P, KT])
                bk = sb(ctx, "bk", [P, D])
                bv = sb(ctx, "bv", [P, D])
                decay_row = sb(ctx, "decay_row", [P, 512])
                decay_col = sb(ctx, "decay_col", [P, T])
                bd_mask = sb(ctx, "bd_mask", [P, P])
                head_mask = sb(ctx, "head_mask", [P, G, 32])
                q_relu = sb(ctx, "q_relu", [P, 2, 512])
                k_biased = sb(ctx, "k_biased", [P, 2, D])
                k_tile = sb(ctx, "k_tile", [P, 2, D])
                v_tile = sb(ctx, "v_tile", [P, 2, G, kv_cols])
                w_loaded = [sem(ctx, f"w5_loaded{i}") for i in range(3)]
                w_hi_ready = sem(ctx, "w5_hi_s")
                w_ready = sem(ctx, "w5_ready")
                small_loaded = sem(ctx, "small_loaded")
                decay_loaded = [sem(ctx, f"decay_loaded{b}") for b in range(NB)]
                proj5 = sem(ctx, "proj5")
                q_relued = sem(ctx, "q_relued")
                read5 = sem(ctx, "read5")
                k_ready = sem(ctx, "k_ready")
                kv_mm = sem(ctx, "kv_mm")
                ones_ready = sem(ctx, "ones5_ready")
                norm = Norm(ctx, "n3_", lambda b, t: x[:, TB * b + t, :], mod_cols[:, 1, SA, :],
                            mod_cols[:, 1, CA, :], ht_hi, ht_lo,
                            used=lambda act, b: act.wait_ge(proj5, (G + 2 * TB) * (b - 1)), zbufs=1)
                PER = G + 2 * TB

                def block_order(b, item, hooks):
                    for m in range(PER):
                        item(b, m)
                        if m in hooks and b + 1 < NB:
                            hooks[m](b + 1)
                with nc.Block() as block:
                    @block.sync
                    def _(sp):
                        for i in range(1, 3):
                            sp.dma_start(w_raw[i], tile_rows(a["w_qkv1"][i])).then_inc(w_loaded[i], 16)
                        sp.dma_start(bq[:], a["bq"]).then_inc(small_loaded, 16)
                        sp.dma_start(bk[:], a["bk"].broadcast_to([P, D])).then_inc(small_loaded, 16)
                        sp.dma_start(bv[:], a["bv"].broadcast_to([P, D])).then_inc(small_loaded, 16)
                        sp.dma_start(decay_col[:], a["decay_col"]).then_inc(small_loaded, 16)
                        sp.dma_start(bd_mask[:], a["const"][:, 6 * P:7 * P]).then_inc(small_loaded, 16)
                        sp.dma_start(head_mask[:], a["const"][:, 7 * P:8 * P].rearrange("p (g e) -> p g e", g=G)).then_inc(small_loaded, 16)
                        sp.wait_ge(w_ready, KT)
                        load_early_projection(sp, a["w_out1"], 1)
                        for b in range(NB):
                            if b:
                                sp.wait_ge(read5, PER * (b - 1) + G)
                            sp.dma_start(decay_row[:], a["decay_row"][:, 512 * b:512 * b + 512].broadcast_to([P, 512])).then_inc(decay_loaded[b], 16)

                    @block.gpsimd
                    def _(pool):
                        for k in range(KT):
                            pool.wait_ge(w_hi_ready, k + 1)
                            nc.gpsimd.tensor_tensor(w_lo[:, 0, k, :], w_raw[0][:, k, :], w_hi[:, 0, k, :],
                                                    ALU.subtract).then_inc(w_ready, 1)

                    @block.tensor
                    def _(pe):
                        def kv_step(i):
                            pe.wait_ge(k_ready, i + 1)
                            pe.wait_ge(read5, PER * (i // TB) + G + 2 * (i % TB) + 2)
                            for g in range(G):
                                first = i == 0 and g % 2 == 0
                                mm = nc.tensor.matmul(bank[6 + g // 2][:, (g % 2) * kv_cols:(g % 2 + 1) * kv_cols],
                                                      k_tile[:, i % 2, P * g:P * g + P], v_tile[:, i % 2, g, :],
                                                      start=first, stop=(i == T - 1), skip_group_check=True)
                            mm.then_inc(kv_mm, 1)

                        def item(b, m):
                            cols, n = norm.cols(b), PER * b + m
                            if n >= 4:
                                pe.wait_ge(read5, n - 3)

                            def chunk_ready(k):
                                pe.wait_ge(norm.ht_ready, KT * b + k + 1)
                                if b == 0:
                                    pe.wait_ge(w_ready, k + 1)
                            dst = bank[2 + n % 4][:]
                            if m < G:
                                c = slice(P * m, P * m + P)
                                mm = product(dst, lambda k: (w_hi[:, 0, k, c], w_lo[:, 0, k, c]),
                                             lambda k: (ht_hi[:, k, cols], ht_lo[:, k, cols]), KT,
                                             before=chunk_ready if m == 0 else None)
                            else:
                                i = 1 + (m - G) % 2
                                if b == 0 and m < G + 2:
                                    pe.wait_ge(w_ready, KT + i)
                                at = cols.start + P * ((m - G) // 2)
                                c = slice(at, at + P)
                                mm = product(dst, lambda k: (ht_hi[:, k, c], ht_lo[:, k, c]),
                                             lambda k: (w_hi[:, i, k, :], w_lo[:, i, k, :]), KT)
                            mm.then_inc(proj5, 1)
                            if m >= G and (m - G) % 2 == 0 and TB * b + (m - G) // 2 >= 1:
                                kv_step(TB * b + (m - G) // 2 - 1)
                        pe.wait_ge(ones_ready, 1)
                        norm.tensor(pe, 0)
                        for b in range(NB):
                            block_order(b, item, {HALF - 1: lambda nb: norm.tensor(pe, nb)})
                        kv_step(T - 1)

                    @block.scalar
                    def _(act):
                        def weights(i):
                            if i == 0:
                                act.wait_ge(early_loaded, QUERY1)
                                for k in range(KT):
                                    nc.scalar.copy(w_hi[:, 0, k, :], w_raw[0][:, k, :]).then_inc(w_hi_ready, 1)
                                return
                            act.wait_ge(w_loaded[i], 16)
                            nc.scalar.copy(w_hi[:, i, :, :], w_raw[i]).then_inc(w_hi_ready, 1)

                        def item(b, m):
                            if m < G:
                                n, e = PER * b + m, G * b + m
                                act.wait_ge(proj5, n + 1)
                                if e >= 2:
                                    act.wait_ge(read5, PER * ((e - 2) // G) + (e - 2) % G + 1)
                                nc.scalar.activation(q_relu[:, e % 2, :], bank[2 + n % 4][:], ACT.Relu,
                                                     bias=bq[:, m:m + 1]).then_inc(q_relued, 1)
                            elif (m - G) % 2 == 0:
                                i = TB * b + (m - G) // 2
                                act.wait_ge(read5, PER * b + m + 1)
                                if i >= 2:
                                    act.wait_ge(kv_mm, i - 1)
                                nc.scalar.activation(k_tile[:, i % 2, :], k_biased[:, i % 2, :], ACT.Relu,
                                                     scale=decay_col[:, i:i + 1]).then_inc(k_ready, 1)
                        weights(0)
                        norm.std_scalar(act, 0)
                        norm.h_scalar(act, 0)
                        weights(1)
                        weights(2)
                        act.wait_ge(small_loaded, 96)
                        for b in range(NB):
                            block_order(b, item, {2: lambda nb: norm.std_scalar(act, nb),
                                                  HALF - 1: lambda nb: norm.h_scalar(act, nb)})

                    @block.vector
                    def _(dve):
                        def weights(i):
                            dve.wait_ge(w_hi_ready, KT + i)
                            dve.wait_ge(w_ready, KT + i - 1)
                            nc.vector.tensor_tensor(w_lo[:, i, :, :], w_raw[i], w_hi[:, i, :, :],
                                                    ALU.subtract).then_inc(w_ready, 1)

                        def item(b, m):
                            n = PER * b + m
                            if m < G:
                                e = G * b + m
                                if m == 0:
                                    dve.wait_ge(decay_loaded[b], 16)
                                if b == 0 and m == 0:
                                    dve.wait_ge(w_ready, KT + 2)
                                dve.wait_ge(q_relued, e + 1)
                                nc.vector.tensor_tensor(qt[:, m, 512 * b:512 * b + 512], q_relu[:, e % 2, :],
                                                        decay_row[:], ALU.mult).then_inc(read5, 1)
                                return
                            i = TB * b + (m - G) // 2
                            dve.wait_ge(proj5, n + 1)
                            if (m - G) % 2 == 0:
                                if i >= 2:
                                    dve.wait_ge(k_ready, i - 1)
                                nc.vector.tensor_tensor(k_biased[:, i % 2, :], bank[2 + n % 4][:], bk[:],
                                                        ALU.add).then_inc(read5, 1)
                            else:
                                if i >= 2:
                                    dve.wait_ge(kv_mm, i - 1)
                                nc.vector.tensor_tensor(v_tile[:, i % 2, :, 0:P],
                                                        bank[2 + n % 4][:].rearrange("p (g e) -> p g e", g=G),
                                                        bv[:].rearrange("p (g e) -> p g e", g=G),
                                                        ALU.add).then_inc(read5, 1)
                        nc.vector.memset(v_tile[:, :, :, P:kv_cols], 1.0).then_inc(ones_ready, 1)
                        norm.stats_vector(dve, 0)
                        norm.z_vector(dve, 0)
                        norm.split_vector(dve, 0)
                        weights(1)
                        weights(2)
                        dve.wait_ge(small_loaded, 96)
                        for b in range(NB):
                            block_order(b, item, {1: lambda nb: norm.stats_vector(dve, nb),
                                                  3: lambda nb: norm.z_vector(dve, nb),
                                                  HALF - 1: lambda nb: norm.split_vector(dve, nb)})
                        dve.wait_ge(kv_mm, T)
                        for g in range(G):
                            src = bank[6 + g // 2][:, (g % 2) * kv_cols:(g % 2 + 1) * kv_cols]
                            nc.vector.tensor_tensor(kv[:, g, :], src[:, 0:P], bd_mask[:], ALU.mult)
                            nc.vector.tensor_scalar(k_sum[:, g, :], head_mask[:, g, :], src[:, P:P + 1], None, ALU.mult)

            h2_hi = sb(ffn, "h3_hi", [P, KT, S], F32R)
            h2_lo = sb(ffn, "h3_lo", [P, KT, S], F32R)
            with ExitStack() as ctx:
                z_hi = sb(ctx, "z_hi", [P, 512], F32R)
                z_lo = sb(ctx, "z_lo", [P, 512], F32R)
                spread = sb(ctx, "spread", [P, NB, G * P], F32R)
                of_block = sb(ctx, "of_block", [P, NB])
                at = qt
                spread_loaded = sem(ctx, "spread_loaded")
                spread_ready = sem(ctx, "spread_ready")
                den_mm = sem(ctx, "den_mm")
                z_step = sem(ctx, "z_step")
                num_mm = sem(ctx, "num_mm")
                num_copied = sem(ctx, "num_copied")
                zb_mm = sem(ctx, "zb_mm")
                at_ready = sem(ctx, "at_ready")
                out_p = project_out(ctx, "o1_", OUT1, (a["gate_wt"], a["up_wt"]), a["b_out1"],
                                    at, lambda act, b: act.wait_ge(at_ready, G * (b + 1)),
                                    lambda pool, t: None)
                norm = Norm(ctx, "n4_", lambda b, t: x[:, TB * b + t, :], mod_cols[:, 1, SB, :],
                            mod_cols[:, 1, CB, :], h2_hi, h2_lo, zbufs=1)
                pattern, z_sum = norm.z[:, 0, 0, :], norm.z[:, 0, 1, :]
                FIRST = 2
                events = [("num", i) for i in range(G * FIRST)] + [("zb", i) for i in range(G)] + \
                         [("num", i) for i in range(G * FIRST, G * NB)] + [("zb", i) for i in range(G, G * NB)]

                def zb_step(pe, i):
                    b, g = divmod(i, G)
                    dst = use_bank(pe, ("zb", i))
                    if i == 0:
                        pe.wait_ge(z_step, 4)
                        pe.wait_ge(spread_ready, NB)
                    nc.tensor.matmul(dst, spread[:, b, P * g:P * g + P], z_hi[:], start=True, stop=False)
                    nc.tensor.matmul(dst, spread[:, b, P * g:P * g + P], z_lo[:], start=False, stop=True).then_inc(zb_mm, 1)

                def bank_of(event):
                    return bank[6 + events.index(event) % 2][:]

                def use_bank(pe, event):
                    e = events.index(event)
                    if e == 1:
                        pe.wait_ge(z_step, 1)
                    elif e >= 2:
                        kind, i = events[e - 2]
                        pe.wait_ge(num_copied if kind == "num" else at_ready, i + 1)
                    return bank_of(event)

                def attend(dve, i):
                    b, g = divmod(i, G)
                    dve.wait_ge(zb_mm, i + 1)
                    dve.wait_ge(num_copied, i + 1)
                    here = at[:, g, 512 * b:512 * b + 512]
                    nc.vector.tensor_tensor(here, bank_of(("zb", i)), here, ALU.mult).then_inc(at_ready, 1)

                def in_two_parts(step):
                    def steps(engine, b, part):
                        for g in (2 * part, 2 * part + 1):
                            step(engine, G * b + g)
                    return steps
                on_tensor, on_scalar, on_vector = projection_and_norm(out_p, norm, in_two_parts(zb_step),
                                                                      in_two_parts(attend))
                with nc.Block() as block:
                    @block.sync
                    def _(sp):
                        out_p.sync(sp)
                        sp.dma_start(pattern, a["spread"][:, 0:G * P]).then_inc(spread_loaded, 16)
                        sp.dma_start(of_block[:], a["spread"][:, G * P:G * P + NB]).then_inc(spread_loaded, 16)
                        out_p.next_sync(sp)

                    @block.gpsimd
                    def _(pool):
                        out_p.bias_gpsimd(pool)

                    @block.tensor
                    def _(pe):
                        for g in range(G):
                            for b in range(NB):
                                last = nc.tensor.matmul(bank[7][32 * b:32 * b + 32, :], k_sum[:, g, :],
                                                        qt[:, g, 512 * b:512 * b + 512],
                                                        start=(g == 0), stop=(g == G - 1))
                        last.then_inc(den_mm, 1)
                        for kind, i in events[:G * (NB + 1)]:
                            if kind == "zb":
                                zb_step(pe, i)
                            else:
                                b, g = divmod(i, G)
                                if i == 0:
                                    pe.wait_ge(den_mm, 1)
                                nc.tensor.matmul(use_bank(pe, (kind, i)), kv[:, g, :], qt[:, g, 512 * b:512 * b + 512],
                                                 start=True, stop=True).then_inc(num_mm, 1)
                        on_tensor(pe)

                    @block.scalar
                    def _(act):
                        def numerator(i):
                            b, g = divmod(i, G)
                            act.wait_ge(num_mm, i + 1)
                            nc.scalar.copy(at[:, g, 512 * b:512 * b + 512], bank_of(("num", i))).then_inc(num_copied, 1)
                        out_p.weights_scalar(act)
                        for i in range(G * FIRST):
                            numerator(i)
                        for i in range(G * FIRST, G * NB):
                            numerator(i)
                        out_p.hi_scalar(act, 0)
                        on_scalar(act)

                    @block.vector
                    def _(dve):
                        out_p.weights_vector(dve)
                        dve.wait_ge(spread_loaded, 32)
                        for b in range(NB):
                            nc.vector.tensor_scalar(spread[:, b, :], pattern, of_block[:, b:b + 1], None,
                                                    ALU.mult).then_inc(spread_ready, 1)
                        dve.wait_ge(den_mm, 1)
                        nc.vector.tensor_scalar(z_sum, bank[7][:], Z_EPS, None, ALU.add).then_inc(z_step, 1)
                        dve.wait_ge(z_step, 1)
                        nc.vector.reciprocal(z_sum, z_sum).then_inc(z_step, 1)
                        dve.wait_ge(z_step, 2)
                        nc.vector.tensor_copy(z_hi[:], z_sum).then_inc(z_step, 1)
                        dve.wait_ge(z_step, 3)
                        nc.vector.tensor_tensor(z_lo[:], z_sum, z_hi[:], ALU.subtract).then_inc(z_step, 1)
                        for i in range(G):
                            attend(dve, i)
                        out_p.lo_vector(dve, 0)
                        dve.wait_ge(spread_ready, NB)
                        dve.wait_ge(z_step, 4)
                        on_vector(dve)

            feed_forward("f1_", 1, FFN1, a["gate_wt"], a["up_wt"], a["down_wt"], H1, (h2_hi, h2_lo),
                         a["gate_s"], a["up_s"], a["down_s"], store=out)


def _constants():
    import numpy as np

    i = np.arange(P)
    eye = np.eye(P, dtype=np.float32)
    signs = np.array([[1.0]], np.float32)
    while signs.shape[0] < P:
        signs = np.block([[signs, signs], [signs, -signs]])
    full = np.full((P, P), MASKED, np.float32)
    later_key = np.where(i[:, None] > i[None, :], np.float32(MASKED), np.float32(0))
    by_key = np.concatenate([full, later_key], 1)
    by_query = np.concatenate([later_key.T, full], 1)
    same_head = (i[:, None] // HD == i[None, :] // HD).astype(np.float32)
    column = np.zeros((P, G, 32), np.float32)
    for g in range(G):
        column[i, g, 4 * g + i // HD] = 1.0
    picks = np.repeat((i % 32 == 0).astype(np.float32)[:, None], P, 1)
    const = np.concatenate([eye, signs, by_key, by_query, same_head, column.reshape(P, -1), picks], 1)
    rows = i[:, None]
    spread = np.concatenate([rows % 32 == 4 * g + i[None, :] // HD for g in range(G)] +
                            [rows // 32 == np.arange(NB)[None, :]], 1).astype(np.float32)
    decay = np.exp(-np.arange(S, dtype=np.float32) / np.float32(S)).astype(np.float32)
    return const.astype(np.float32), spread, decay


def kernel(**inputs):
    import numpy as np
    import concourse.bacc as bacc
    from concourse.bass_utils import run_bass_kernel_spmd

    const, spread, decay = _constants()
    w = np.asarray(inputs["L0_attn_W_qkv"]).reshape(D, HEADS, 3, HD)
    b = np.asarray(inputs["L0_attn_b_qkv"]).reshape(HEADS, 3, HD)
    flat = lambda m: np.asarray(m).reshape(-1, P).T
    row = lambda m: np.asarray(m).reshape(1, -1)
    arrays = {
        "L0_attn_x": np.asarray(inputs["L0_attn_x"])[0],
        "w_qkv": w.transpose(2, 0, 1, 3).reshape(3, D, D),
        "qk_bias": np.concatenate([flat(b[:, 0]), flat(b[:, 1])], 1),
        "v_bias": row(b[:, 2]),
        "w_out0": inputs["L0_attn_W_out"], "b_out0": row(inputs["L0_attn_b_out"]),
        "w1t": np.asarray(inputs["L0_ffn_W1"]).T, "w3t": np.asarray(inputs["L0_ffn_W3"]).T,
        "w2t": np.asarray(inputs["L0_ffn_W2"]).T,
        "L0_c": flat(inputs["L0_c"]), "L0_wmod": inputs["L0_wmod"], "L1_c": flat(inputs["L1_c"]), "L1_wmod": inputs["L1_wmod"],
        "w_qkv1": np.stack([np.asarray(inputs[f"L1_attn_W{n}"]).T for n in "qkv"]),
        "bq": flat(inputs["L1_attn_bq"]), "bk": row(inputs["L1_attn_bk"]), "bv": row(inputs["L1_attn_bv"]),
        "w_out1": np.asarray(inputs["L1_attn_Wo"]).T, "b_out1": row(inputs["L1_attn_bo"]),
        "gate_wt": np.asarray(inputs["L1_ffn_gate_w"]).T, "up_wt": np.asarray(inputs["L1_ffn_up_w"]).T,
        "down_wt": np.asarray(inputs["L1_ffn_down_w"]).T,
        "gate_s": flat(inputs["L1_ffn_gate_s"]), "up_s": flat(inputs["L1_ffn_up_s"]),
        "down_s": row(inputs["L1_ffn_down_s"]),
        "const": const, "spread": spread, "decay_row": decay.reshape(1, S), "decay_col": decay.reshape(T, P).T,
    }
    nc = bacc.Bacc("TRN2", target_bir_lowering=False, num_devices=1)
    fed, aps = {}, {}
    for name, m in arrays.items():
        m = np.ascontiguousarray(m)
        fed[f"in_{name}"] = m
        aps[name] = nc.dram_tensor(f"in_{name}", m.shape, mybir.dt.from_np(m.dtype), kind="ExternalInput").ap()
    out = nc.dram_tensor("out", (S, D), F32, kind="ExternalOutput").ap()
    build_program(nc, aps, out)
    r = run_bass_kernel_spmd(nc, [fed], core_ids=[0])
    return r.results[0]["out"].reshape(1, S, D)
```
